# Optimizing a Trainium2 kernel written in Bass

```python
import numpy as np
import jax
import jax.numpy as jnp

def _softmax(x, axis=-1):
    return jax.nn.softmax(x, axis=axis)

def _gelu(x):
    return jax.nn.gelu(x, approximate=True)

def _silu(x):
    return jax.nn.silu(x)

def _sigmoid(x):
    return jax.nn.sigmoid(x)

def _layernorm(x, axis=-1, eps=1e-05):
    m = jnp.mean(x, axis=axis, keepdims=True)
    v = jnp.var(x, axis=axis, keepdims=True)
    return (x - m) / jnp.sqrt(v + eps)

def _scatter_add(tgt, idx, src, axis=0):
    return tgt.at[idx].add(src)

def _segment_sum(src, seg, n):
    return jax.ops.segment_sum(src, seg, n)
kernel_name = 'mk_flamingo_gated_d1_seqx_r4_3a1bd9'

def setup_inputs(seed: int=0):
    np.random.seed(seed)
    _w = jnp.asarray

    def _rec_inputs():
        import jax
        import jax.numpy as jnp
        _rk = jax.random.key(seed)
        x = 0.002226 + 0.9996 * jax.random.normal(jax.random.fold_in(_rk, 1), (16, 256, 256), jnp.float32)
        _lenS = 256 - jax.random.randint(jax.random.fold_in(_rk, 7), (16,), 0, max(1, 256 // 4) + 1, jnp.int32)
        _lenS2 = 77 - jax.random.randint(jax.random.fold_in(_rk, 8), (16,), 0, max(1, 77 // 4) + 1, jnp.int32)
        _ctx_1024P = jax.random.normal(jax.random.fold_in(_rk, 11), (16, 16, 256), jnp.float32)
        _ctx_1024c = jax.random.dirichlet(jax.random.fold_in(_rk, 511), 0.3 * jnp.ones((16,), jnp.float32), (16, 77))
        _ctx_1024t = jnp.einsum('bsk,bkd->bsd', _ctx_1024c, _ctx_1024P)
        _ctx_1024t = _ctx_1024t * jax.lax.rsqrt(jnp.mean(jnp.square(_ctx_1024t)) + 1e-12) * 0.953939
        ctx_1024 = -0.000125008 + 0.999885 * (_ctx_1024t + 0.3 * jax.random.normal(jax.random.fold_in(_rk, 611), (16, 77, 256), jnp.float32))
        _g = jax.random.normal(jax.random.fold_in(_rk, 9001), (2, 1), jnp.float32)
        _g = jnp.sign(_g) * jnp.maximum(jnp.abs(_g), 1.0) + (_g == 0) * 1.0
        g_xattn = _g[0]
        g_ffn = _g[1]
        return (x, ctx_1024, g_xattn, g_ffn)
    x, ctx_1024, g_xattn, g_ffn = _rec_inputs()

    def _L0_xattn_setup():
        import jax, jax.numpy as jnp
        import numpy as np
        B, M, N, DIM, DH, H = (8, 1024, 64, 256, 128, 8)
        INNER = DH * H
        EPS = 1e-05

        def _layernorm(x, g, b):
            mu = jnp.mean(x, axis=-1, keepdims=True)
            var = jnp.var(x, axis=-1, keepdims=True)
            return (x - mu) * jax.lax.rsqrt(var + EPS) * g + b
        key = jax.random.key(seed)
        ks = jax.random.split(key, 8)
        sd = 0.02
        return {'x': jax.random.normal(ks[0], (B, M, DIM), jnp.float32), 'latents': jax.random.normal(ks[1], (B, N, DIM), jnp.float32), 'gamma_media': jnp.ones((DIM,), jnp.float32), 'beta_media': jnp.zeros((DIM,), jnp.float32), 'gamma_lat': jnp.ones((DIM,), jnp.float32), 'beta_lat': jnp.zeros((DIM,), jnp.float32), 'Wq': jax.random.normal(ks[2], (DIM, INNER), jnp.float32) * sd, 'bq': jnp.zeros((INNER,), jnp.float32), 'Wkv': jax.random.normal(ks[3], (DIM, 2 * INNER), jnp.float32) * sd, 'bkv': jnp.zeros((2 * INNER,), jnp.float32), 'Wo': jax.random.normal(ks[4], (INNER, DIM), jnp.float32) * sd, 'bo': jnp.zeros((DIM,), jnp.float32)}
    _L0_xattn_all = _L0_xattn_setup()
    _L0_xattn_in = {k: v for k, v in _L0_xattn_all.items() if k in ('gamma_media', 'beta_media', 'gamma_lat', 'beta_lat', 'Wq', 'bq', 'Wkv', 'bkv', 'Wo', 'bo')}
    del _L0_xattn_all

    def _L0_ffn_setup():
        import jax, jax.numpy as jnp
        import numpy as np
        B, S, H = (2, 1024, 256)
        I = 128
        E = 8
        TOPK = 2
        NGROUP = 2
        TOPK_GROUP = 1
        ROUTED_SCALE = 1.0

        def _silu(x):
            return x * jax.nn.sigmoid(x)
        key = jax.random.key(seed)
        ks = jax.random.split(key, 9)

        def w(k, shape, s=0.05):
            return jax.random.normal(k, shape, dtype=jnp.float32) * s
        return {'hidden_states': jax.random.normal(ks[0], (B, S, H), dtype=jnp.float32), 'router_weight': w(ks[1], (E, H)), 'correction_bias': w(ks[2], (E,)), 'w_gate': w(ks[3], (E, H, I)), 'w_up': w(ks[4], (E, H, I)), 'w_down': w(ks[5], (E, I, H)), 'sw_gate': w(ks[6], (H, I)), 'sw_up': w(ks[7], (H, I)), 'sw_down': w(ks[8], (I, H))}
    _L0_ffn_all = _L0_ffn_setup()
    _L0_ffn_in = {k: v for k, v in _L0_ffn_all.items() if k in ('router_weight', 'correction_bias', 'w_gate', 'w_up', 'w_down', 'sw_gate', 'sw_up', 'sw_down')}
    del _L0_ffn_all
    return {'x': x, 'ctx_1024': ctx_1024, 'g_xattn': g_xattn, 'g_ffn': g_ffn, 'L0_xattn_gamma_media': _L0_xattn_in['gamma_media'], 'L0_xattn_beta_media': _L0_xattn_in['beta_media'], 'L0_xattn_gamma_lat': _L0_xattn_in['gamma_lat'], 'L0_xattn_beta_lat': _L0_xattn_in['beta_lat'], 'L0_xattn_Wq': _L0_xattn_in['Wq'], 'L0_xattn_bq': _L0_xattn_in['bq'], 'L0_xattn_Wkv': _L0_xattn_in['Wkv'], 'L0_xattn_bkv': _L0_xattn_in['bkv'], 'L0_xattn_Wo': _L0_xattn_in['Wo'], 'L0_xattn_bo': _L0_xattn_in['bo'], 'L0_ffn_router_weight': _L0_ffn_in['router_weight'], 'L0_ffn_correction_bias': _L0_ffn_in['correction_bias'], 'L0_ffn_w_gate': _L0_ffn_in['w_gate'], 'L0_ffn_w_up': _L0_ffn_in['w_up'], 'L0_ffn_w_down': _L0_ffn_in['w_down'], 'L0_ffn_sw_gate': _L0_ffn_in['sw_gate'], 'L0_ffn_sw_up': _L0_ffn_in['sw_up'], 'L0_ffn_sw_down': _L0_ffn_in['sw_down']}

def reference(x, ctx_1024, g_xattn, g_ffn, L0_xattn_gamma_media, L0_xattn_beta_media, L0_xattn_gamma_lat, L0_xattn_beta_lat, L0_xattn_Wq, L0_xattn_bq, L0_xattn_Wkv, L0_xattn_bkv, L0_xattn_Wo, L0_xattn_bo, L0_ffn_router_weight, L0_ffn_correction_bias, L0_ffn_w_gate, L0_ffn_w_up, L0_ffn_w_down, L0_ffn_sw_gate, L0_ffn_sw_up, L0_ffn_sw_down):
    import jax
    import jax.numpy as jnp

    def _L0_xattn_ref(x, latents, gamma_media, beta_media, gamma_lat, beta_lat, Wq, bq, Wkv, bkv, Wo, bo):
        import jax, jax.numpy as jnp
        import numpy as np
        B, M, N, DIM, DH, H = (8, 1024, 64, 256, 128, 8)
        INNER = DH * H
        EPS = 1e-05

        def _layernorm(x, g, b):
            mu = jnp.mean(x, axis=-1, keepdims=True)
            var = jnp.var(x, axis=-1, keepdims=True)
            return (x - mu) * jax.lax.rsqrt(var + EPS) * g + b
        b = x.shape[0]
        xn = _layernorm(x, gamma_media, beta_media)
        ln = _layernorm(latents, gamma_lat, beta_lat)
        q = ln @ Wq + bq
        kv_input = jnp.concatenate([xn, ln], axis=1)
        kv = kv_input @ Wkv + bkv
        k, v = jnp.split(kv, 2, axis=-1)

        def to_heads(t):
            return t.reshape(b, t.shape[1], H, DH).transpose(0, 2, 1, 3)
        q, k, v = (to_heads(q), to_heads(k), to_heads(v))
        q = q * DH ** (-0.5)
        sim = jnp.einsum('bhid,bhjd->bhij', q, k)
        attn = jax.nn.softmax(sim, axis=-1)
        out = jnp.einsum('bhij,bhjd->bhid', attn, v)
        out = out.transpose(0, 2, 1, 3).reshape(b, -1, INNER)
        return out @ Wo + bo

    def _L0_ffn_ref(hidden_states, router_weight, correction_bias, w_gate, w_up, w_down, sw_gate, sw_up, sw_down):
        import jax, jax.numpy as jnp
        import numpy as np
        B, S, H = (2, 1024, 256)
        I = 128
        E = 8
        TOPK = 2
        NGROUP = 2
        TOPK_GROUP = 1
        ROUTED_SCALE = 1.0

        def _silu(x):
            return x * jax.nn.sigmoid(x)
        b, s, h = hidden_states.shape
        x = hidden_states.reshape(-1, h)
        logits = x @ router_weight.T
        scores = jax.nn.sigmoid(logits)
        scores_for_choice = scores + correction_bias[None, :]
        e_per_g = E // NGROUP
        group_scores = jax.lax.top_k(scores_for_choice.reshape(-1, NGROUP, e_per_g), 2)[0].sum(-1)
        group_idx = jax.lax.top_k(group_scores, TOPK_GROUP)[1]
        group_mask = jax.nn.one_hot(group_idx, NGROUP, dtype=scores.dtype).sum(1)
        score_mask = jnp.repeat(group_mask, e_per_g, axis=1)
        masked = jnp.where(score_mask > 0, scores_for_choice, 0.0)
        topk_idx = jax.lax.top_k(masked, TOPK)[1]
        topk_w = jnp.take_along_axis(scores, topk_idx, axis=1)
        topk_w = topk_w / (topk_w.sum(-1, keepdims=True) + 1e-20)
        topk_w = topk_w * ROUTED_SCALE
        comb = (jax.nn.one_hot(topk_idx, E, dtype=x.dtype) * topk_w[..., None]).sum(1)
        g = jnp.einsum('th,ehi->tei', x, w_gate)
        u = jnp.einsum('th,ehi->tei', x, w_up)
        y = jnp.einsum('tei,eih->teh', _silu(g) * u, w_down)
        routed = jnp.einsum('teh,te->th', y, comb).reshape(b, s, h)
        shared = _silu(hidden_states @ sw_gate) * (hidden_states @ sw_up) @ sw_down
        return routed + shared
    x = x + jnp.tanh(g_xattn[0]) * _L0_xattn_ref(ctx_1024, _layernorm(x, axis=-1), L0_xattn_gamma_media, L0_xattn_beta_media, L0_xattn_gamma_lat, L0_xattn_beta_lat, L0_xattn_Wq, L0_xattn_bq, L0_xattn_Wkv, L0_xattn_bkv, L0_xattn_Wo, L0_xattn_bo)
    x = x + jnp.tanh(g_ffn[0]) * _L0_ffn_ref(_layernorm(x, axis=-1), L0_ffn_router_weight, L0_ffn_correction_bias, L0_ffn_w_gate, L0_ffn_w_up, L0_ffn_w_down, L0_ffn_sw_gate, L0_ffn_sw_up, L0_ffn_sw_down)
    return x

_drawn_inputs = setup_inputs


def setup_inputs(seed=0):
    import zlib

    import numpy as np

    out = dict(_drawn_inputs(seed))
    spreads = {'L0_xattn_gamma_media': (1.0, 0.6),
     'L0_xattn_beta_media': (0.0, 0.799),
     'L0_xattn_gamma_lat': (1.0, 0.6),
     'L0_xattn_beta_lat': (0.0, 0.358),
     'L0_xattn_bq': (0.0, 2.0),
     'L0_xattn_bkv': (0.0, 0.1),
     'L0_xattn_bo': (0.0, 0.1)}
    factors = {'L0_xattn_Wq': 8.0}
    for name, (base, spread) in spreads.items():
        noise = np.random.default_rng([zlib.crc32(name.encode()), seed]).standard_normal(out[name].shape)
        drawn = base * np.exp(spread * noise) if base else spread * noise
        out[name] = jnp.asarray(drawn.astype(out[name].dtype))
    for name, factor in factors.items():
        out[name] = (out[name] * factor).astype(out[name].dtype)
    return out
```

```python
from contextlib import ExitStack

import concourse.bass as bass
from concourse import mybir

F32 = mybir.dt.float32
F32R = mybir.dt.float32r
ALU = mybir.AluOpType
ACT = mybir.ActivationFunctionType
AX = mybir.AxisListType

P = 128
EPS = 1e-5
BATCH, TOK, DIM = 16, 256, 256
MEDIA = 77
HEADS, DH = 8, 128
INNER = HEADS * DH
KEYS = TOK + MEDIA
KPAD = KEYS + 1
FC = DIM // P
TT = TOK // P
STEPS = BATCH * HEADS
VGROUPS = 6
VG_AT = {0: (0, 1), 1: (2,), 2: (3,), 3: (4,), 4: (5,)}
SCALE = float(DH) ** -0.5

EXP, I = 8, 128
UNITS = 3
UN = (4, 4, 1)
UE = (0, 4, 8)
RAW = 3 * FC * INNER + HEADS * DIM
GU = 2 * (EXP + 1) * I + EXP
RAW_DMAS = 14
PAIRS = BATCH


def _wait(engine, sem, n):
    if not isinstance(n, int) or n > 0:
        engine.wait_ge(sem, n)


def _live(n, end):
    return not isinstance(n, int) or 0 <= n < end


def attention(nc, t, x_all, ident, raw, load_ffn):
    with ExitStack() as ctx:
        def sb(name, shape, dt=F32):
            return ctx.enter_context(nc.sbuf_tensor(name, shape, dt))

        def ps(name, shape):
            return ctx.enter_context(nc.psum_tensor(name, shape, F32))

        def sem(name):
            return ctx.enter_context(nc.semaphore(name))

        QO, KVO, OO = 0, FC * INNER, 3 * FC * INNER
        WN = OO + HEADS * DIM
        w_hi = sb("w_hi", [P, WN], F32R)
        w_lo = sb("w_lo", [P, WN], F32R)
        def piece(w, n):
            if n == 0:
                return w[:, QO:KVO].rearrange("p (c n) -> p c n", c=FC)
            if n == 3:
                return w[:, OO:WN].rearrange("p (c n) -> p c n", c=HEADS)
            return w[:, KVO:OO].rearrange("p (c n) -> p c n", c=FC)[:, :, (n - 1) * INNER:n * INNER]

        def wq(w, c, h):
            return piece(w, 0)[:, c, h * DH:(h + 1) * DH]

        def wk(w, c, h):
            return piece(w, 1)[:, c, h * DH:(h + 1) * DH]

        def wv(w, c, half):
            return piece(w, 2)[:, c, half * 512:(half + 1) * 512]

        def wo(w, h):
            return piece(w, 3)[:, h, :]

        gb = sb("gb", [P, 4, FC])
        bq = sb("bq", [P, HEADS])
        bqs = sb("bqs", [P, HEADS])
        bkv = sb("bkv", [P, 2 * HEADS])
        bo = sb("bo", [P, DIM])
        tgbo = sb("tgbo", [P, DIM])
        gx = sb("gx", [P, 1])
        tg = sb("tg", [P, 1])
        ctx_in = sb("ctx_in", [MEDIA, DIM])
        stats = sb("stats", [P, 3, 6])
        mv = sb("mv", [P, 3, 2])
        rs = sb("rs", [P, 5, 3])
        mhalf = sb("mhalf", [P, 3])
        eps3 = sb("eps3", [P, 3])
        z = sb("z", [P, 3, DIM])
        lnf = sb("lnf", [P, FC, KPAD])
        ln_hi = sb("ln_hi", [P, FC, KPAD], F32R)
        ln_lo = sb("ln_lo", [P, FC, KPAD], F32R)
        q_hi = sb("q_hi", [P, 2, TOK], F32R)
        q_lo = sb("q_lo", [P, 2, TOK], F32R)
        k_hi = sb("k_hi", [P, 2, KPAD], F32R)
        k_lo = sb("k_lo", [P, 2, KPAD], F32R)
        v_hi = sb("v_hi", [P, 2, 3, 512], F32R)
        v_lo = sb("v_lo", [P, 2, 3, 512], F32R)
        prob = sb("prob", [P, 2, TT, KPAD])
        nmax = sb("nmax", [P, 2, TT])
        rsum = sb("rsum", [P, 2, TT])
        rinv = sb("rinv", [P, 2, TT])
        pt_hi = sb("pt_hi", [P, 2, 3 * TOK], F32R)
        pt_lo = sb("pt_lo", [P, 2, 3 * TOK], F32R)
        o_hi = sb("o_hi", [P, 2, TOK], F32R)
        o_lo = sb("o_lo", [P, 2, TOK], F32R)

        ps_s = [ps("ps_s0", [P, 512]), ps("ps_s1", [P, 512])]
        ps_qa = ps("ps_qa", [P, 512])
        ps_k = ps("ps_k", [P, 512])
        ps_v = ps("ps_v", [P, 512])
        ps_t = ps("ps_t", [P, 1024])
        ps_y = ps("ps_y", [P, 512])

        x_in = [sem("x_in0"), sem("x_in1")]
        vec_in, media_in = sem("vec_in"), sem("media_in")
        w_in = [sem(f"w_in{n}") for n in range(4)]
        id_ready, const_ready, tg_ready = sem("id_ready"), sem("const_ready"), sem("tg_ready")
        bias_ready, half_ready = sem("bias_ready"), sem("half_ready")
        whi_ready, wlo_ready = sem("whi_ready"), sem("wlo_ready")
        stats_ready, rstd_ready, rstd_step, z_ready = sem("stats_ready"), sem("rstd_ready"), sem("rstd_step"), sem("z_ready")
        bn_ready = sem("bn_ready")
        tok_turned, tok_scaled, lnhi_ready, lnlo_ready = sem("tok_turned"), sem("tok_scaled"), sem("lnhi_ready"), sem("lnlo_ready")
        qk_projected, qhi_ready, khi_ready, qklo_ready = sem("qk_projected"), sem("qhi_ready"), sem("khi_ready"), sem("qklo_ready")
        v_projected, vhi_ready, vlo_ready = sem("v_projected"), sem("vhi_ready"), sem("vlo_ready")
        scored, max_ready, exp_ready, rinv_ready = sem("scored"), sem("max_ready"), sem("exp_ready"), sem("rinv_ready")
        norm0_ready, norm1_ready = sem("norm0_ready"), sem("norm1_ready")
        p_turned, pthi_ready, ptlo_ready = sem("p_turned"), sem("pthi_ready"), sem("ptlo_ready")
        attended, ohi_ready, olo_ready = sem("attended"), sem("ohi_ready"), sem("olo_ready")
        projected, xb_ready, x2_ready = sem("projected"), sem("xb_ready"), sem("x2_ready")

        block = ctx.enter_context(nc.Block())

        @block.sync
        def _(sp):
            x_tiles = t["x"].rearrange("b (i p) d -> p (b i) d", p=P)
            sp.dma_start(x_all[:, 0:TT, :], x_tiles[:, 0:TT, :]).then_inc(x_in[0], 16)
            sp.dma_start(ctx_in[:, :], t["ctx_1024"][0]).then_inc(media_in, 16)
            sp.dma_start(piece(raw, 0), t["L0_xattn_Wq"].rearrange("(c p) n -> p c n", p=P)).then_inc(w_in[0], 16)
            kv = t["L0_xattn_Wkv"].rearrange("(c p) n -> p c n", p=P)
            for n in (1, 2):
                sp.dma_start(piece(raw, n), kv[:, :, (n - 1) * INNER:n * INNER]).then_inc(w_in[n], 16)
            sp.dma_start(piece(raw, 3), t["L0_xattn_Wo"].rearrange("(c p) n -> p c n", p=P)).then_inc(w_in[3], 16)
            sp.dma_start(x_all[:, TT:, :], x_tiles[:, TT:, :]).then_inc(x_in[1], 16)
            sp.wait_ge(wlo_ready, 4)
            load_ffn(sp)
            with sp.Fori(1, BATCH) as b:
                sp.wait_ge(z_ready, 3 * b)
                sp.dma_start(ctx_in[:, :], t["ctx_1024"][bass.ds(b, 1)].rearrange("o j d -> (o j) d")).then_inc(media_in, 16)

        @block.gpsimd
        def _(pool):
            pool.memset(ident[:, :], 0.0).then_inc(id_ready, 1)
            pool.memset(mhalf[:, :], -0.5).then_inc(half_ready, 1)
            pool.memset(eps3[:, :], EPS).then_inc(half_ready, 1)
            pool.wait_ge(id_ready, 1)
            pool.affine_select(out=ident[:, :], in_=ident[:, :], compare_op=ALU.not_equal, fill=1.0, base=0,
                               pattern=[[-1, P]], channel_multiplier=1).then_inc(id_ready, 1)

            def reciprocal_deviations(b):
                ve, r1, sq, ve2, rr = (rs[:, n, :] for n in range(5))
                pool.wait_ge(stats_ready, 3 * (b + 1))
                _wait(pool, z_ready, 3 * b)
                pool.wait_ge(half_ready, 2)
                var = mv[:, :, 1]
                pool.tensor_tensor(ve, var, eps3[:, :], ALU.add).then_inc(rstd_step, 1)
                pool.wait_ge(rstd_step, 6 * b + 1)
                pool.tensor_tensor(r1, ve, mhalf[:, :], ALU.pow).then_inc(rstd_step, 1)
                pool.wait_ge(rstd_step, 6 * b + 2)
                pool.tensor_tensor(sq, r1, r1, ALU.mult).then_inc(rstd_step, 1)
                pool.wait_ge(rstd_step, 6 * b + 3)
                pool.tensor_tensor(sq, sq, var, ALU.mult).then_inc(rstd_step, 1)
                pool.wait_ge(rstd_step, 6 * b + 4)
                pool.tensor_tensor(ve2, sq, eps3[:, :], ALU.add).then_inc(rstd_step, 1)
                pool.wait_ge(rstd_step, 6 * b + 5)
                pool.tensor_tensor(sq, ve2, mhalf[:, :], ALU.pow).then_inc(rstd_step, 1)
                pool.wait_ge(rstd_step, 6 * b + 6)
                pool.tensor_tensor(rr, r1, sq, ALU.mult).then_inc(rstd_ready, 1)

            def step(b, h):
                s = HEADS * b + h
                pool.wait_ge(rinv_ready, s + 1)
                pool.tensor_tensor(prob[:, h % 2, 0, 0:KEYS], prob[:, h % 2, 0, 0:KEYS],
                                   rinv[:, h % 2, 0:1].to_broadcast([P, KEYS]), ALU.mult).then_inc(norm0_ready, 1)
                if h == 1 and _live(b + 1, BATCH):
                    reciprocal_deviations(b + 1)
                if h == 4:
                    rows = x_all[:, bass.ds(TT * b, TT), :]
                    pool.wait_ge(z_ready, 3 * (b + 1))
                    pool.wait_ge(tg_ready, 2)
                    pool.tensor_tensor(rows, rows, tgbo[:, :].unsqueeze(1).to_broadcast([P, TT, DIM]),
                                       ALU.add).then_inc(xb_ready, 1)

            reciprocal_deviations(0)
            for h in range(HEADS):
                step(0, h)
            with pool.Fori(1, BATCH - 1) as b:
                for h in range(HEADS):
                    step(b, h)
            for h in range(HEADS):
                step(BATCH - 1, h)

        @block.scalar
        def _(act):
            act.dma_start(gx[:, :], t["g_xattn"].unsqueeze(0).to_broadcast([P, 1])).then_inc(vec_in, 16)
            for n, name in enumerate(("gamma_lat", "beta_lat", "gamma_media", "beta_media")):
                act.dma_start(gb[:, n, :], t["L0_xattn_" + name].rearrange("(c p) -> p c", p=P),
                              allow_slow_non_contiguous=True).then_inc(vec_in, 16)
            act.dma_start(bq[:, :], t["L0_xattn_bq"].rearrange("(h p) -> p h", p=P),
                          allow_slow_non_contiguous=True).then_inc(vec_in, 16)
            act.dma_start(bkv[:, :], t["L0_xattn_bkv"].rearrange("(h p) -> p h", p=P),
                          allow_slow_non_contiguous=True).then_inc(vec_in, 16)
            act.dma_start(bo[:, :], t["L0_xattn_bo"].unsqueeze(0).to_broadcast([P, DIM])).then_inc(vec_in, 16)
            act.wait_ge(vec_in, 16 * 8)
            act.activation(tg[:, :], gx[:, :], ACT.Tanh).then_inc(tg_ready, 1)
            act.activation(bqs[:, :], bq[:, :], ACT.Copy, scale=SCALE).then_inc(bias_ready, 1)

            def turned_tokens(b, c):
                act.wait_ge(tok_turned, FC * b + c + 1)
                _wait(act, lnlo_ready, b)
                act.activation(lnf[:, c, 0:TOK], ps_v[:, 0:TOK], ACT.Identity, bias=gb[:, 1, c:c + 1],
                               scale=gb[:, 0, c:c + 1]).then_inc(tok_scaled, 1)
                act.activation(lnf[:, c, TOK:KEYS], ps_v[:, TOK:KEYS], ACT.Identity, bias=gb[:, 3, c:c + 1],
                               scale=gb[:, 2, c:c + 1]).then_inc(tok_scaled, 1)

            def tokens_hi(b):
                act.wait_ge(tok_scaled, 2 * FC * (b + 1))
                _wait(act, qk_projected, 2 * HEADS * b)
                _wait(act, v_projected, VGROUPS * b)
                act.activation(ln_hi[:, :, :], lnf[:, :, :], ACT.Copy).then_inc(lnhi_ready, 1)

            def qk_hi(u, par, h):
                act.wait_ge(qk_projected, 2 * u + 1)
                _wait(act, scored, 2 * (u - 1))
                act.activation(q_hi[:, par, :], ps_qa[:, 0:TOK], ACT.Identity,
                               bias=bqs[:, h:h + 1]).then_inc(qhi_ready, 1)
                act.wait_ge(qk_projected, 2 * u + 2)
                act.activation(k_hi[:, par, :], ps_k[:, 0:KPAD], ACT.Identity,
                               bias=bkv[:, h:h + 1]).then_inc(khi_ready, 1)

            def v_piece(b, g):
                half, j = divmod(g, 3)
                act.wait_ge(v_projected, VGROUPS * b + g + 1)
                _wait(act, attended, HEADS * b - 4 + 4 * half)
                rows = P if j < 2 else MEDIA
                act.activation(v_hi[0:rows, half, j, :], ps_v[0:rows, :], ACT.Copy).then_inc(vhi_ready, 1)

            def step(b, h):
                s = HEADS * b + h
                if _live(s, STEPS):
                    for i in range(TT):
                        act.wait_ge(max_ready, 2 * s + i + 1)
                        _wait(act, p_turned, s - 1)
                        act.activation(prob[:, h % 2, i, 0:KEYS], ps_s[i][:, 0:KEYS], ACT.Exp,
                                       bias=nmax[:, h % 2, i:i + 1],
                                       accum_out=rsum[:, h % 2, i:i + 1]).then_inc(exp_ready, 1)
                if _live(s - 1, STEPS):
                    act.wait_ge(p_turned, s)
                    _wait(act, attended, s - 2)
                    act.activation(pt_hi[:, (h - 1) % 2, :], ps_t[:, 0:3 * TOK], ACT.Copy).then_inc(pthi_ready, 1)
                if _live(s + 1, STEPS):
                    qk_hi(s + 1, (h + 1) % 2, (h + 1) % HEADS)
                if _live(s, STEPS):
                    if h == 6 and _live(b + 1, BATCH):
                        tokens_hi(b + 1)
                    for g in VG_AT.get(h, ()):
                        v_piece(b, g)
                    if h in (4, 5) and _live(b + 1, BATCH):
                        turned_tokens(b + 1, h - 4)
                if _live(s - 2, STEPS):
                    hh = (h - 2) % HEADS
                    act.wait_ge(attended, s - 1)
                    _wait(act, projected, s - 3)
                    act.activation(o_hi[:, h % 2, :], ps_qa[:, TOK:2 * TOK], ACT.Identity,
                                   bias=bkv[:, HEADS + hh:HEADS + hh + 1]).then_inc(ohi_ready, 1)

            for n in range(4):
                if n == 1:
                    act.wait_ge(const_ready, 2)
                    for c in range(FC):
                        turned_tokens(0, c)
                    tokens_hi(0)
                act.wait_ge(w_in[n], 16)
                act.activation(piece(w_hi, n), piece(raw, n), ACT.Copy,
                               scale=SCALE if n == 0 else 1.0).then_inc(whi_ready, 1)
                if n == 1:
                    act.wait_ge(bias_ready, 1)
                    qk_hi(0, 0, 0)
            for h in range(HEADS):
                step(0, h)
            with act.Fori(1, BATCH - 1) as b:
                for h in range(HEADS):
                    step(b, h)
            for h in range(HEADS):
                step(BATCH - 1, h)
            for h in range(3):
                step(BATCH, h)

        @block.vector
        def _(dve):
            dve.memset(mv[:, :, :], 1.0).then_inc(bn_ready, 1)
            dve.memset(lnf[:, :, KEYS:KPAD], 0.0).then_inc(const_ready, 1)
            dve.memset(ps_t[:, :], 0.0).then_inc(const_ready, 1)

            def statistics(b):
                if not isinstance(b, int) or b > 0:
                    dve.wait_ge(x_in[1], 16)
                else:
                    dve.wait_ge(x_in[0], 16)
                for i in range(TT):
                    dve.bn_stats(stats[:, i, :], x_all[:, bass.ds(TT * b + i, 1), :].rearrange("p o d -> p (o d)"))\
                       .then_inc(bn_ready, 1)
                dve.wait_ge(media_in, 16 * (b + 1))
                dve.bn_stats(stats[0:MEDIA, 2, :], ctx_in[:, :]).then_inc(bn_ready, 1)

            def aggregate(b):
                for i in range(3):
                    rows = P if i < 2 else MEDIA
                    dve.bn_aggr(mv[0:rows, i, :], stats[0:rows, i, :]).then_inc(stats_ready, 1)

            def normalise(b):
                dve.wait_ge(rstd_ready, b + 1)
                _wait(dve, tok_turned, FC * b)
                for i in range(TT):
                    dve.tensor_scalar(z[:, i, :], x_all[:, bass.ds(TT * b + i, 1), :].rearrange("p o d -> p (o d)"),
                                      mv[:, i, 0:1], rs[:, 4, i:i + 1], ALU.subtract, ALU.mult).then_inc(z_ready, 1)
                dve.tensor_scalar(z[0:MEDIA, 2, :], ctx_in[:, :], mv[0:MEDIA, 2, 0:1], rs[0:MEDIA, 1, 2:3],
                                  ALU.subtract, ALU.mult).then_inc(z_ready, 1)

            def tokens_lo(b):
                dve.wait_ge(lnhi_ready, b + 1)
                dve.tensor_tensor(ln_lo[:, :, :], lnf[:, :, :], ln_hi[:, :, :].bitcast(F32),
                                  ALU.subtract).then_inc(lnlo_ready, 1)

            def qk_lo(u, par, h):
                dve.wait_ge(qhi_ready, u + 1)
                dve.scalar_tensor_tensor(out=q_lo[:, par, :], in0=ps_qa[:, 0:TOK], scalar=bqs[:, h:h + 1],
                                         in1=q_hi[:, par, :].bitcast(F32), op0=ALU.add,
                                         op1=ALU.subtract).then_inc(qklo_ready, 1)
                dve.wait_ge(khi_ready, u + 1)
                dve.scalar_tensor_tensor(out=k_lo[:, par, :], in0=ps_k[:, 0:KPAD], scalar=bkv[:, h:h + 1],
                                         in1=k_hi[:, par, :].bitcast(F32), op0=ALU.add,
                                         op1=ALU.subtract).then_inc(qklo_ready, 1)

            def step(b, h):
                s = HEADS * b + h
                if _live(s, STEPS):
                    for i in range(TT):
                        dve.wait_ge(scored, 2 * s + i + 1)
                        _wait(dve, exp_ready, 2 * (s - 1))
                        dve.tensor_reduce(nmax[:, h % 2, i:i + 1], ps_s[i][:, 0:KEYS], AX.X, ALU.max,
                                          negate=True).then_inc(max_ready, 1)
                    if h == 0 and _live(b + 1, BATCH):
                        statistics(b + 1)
                        dve.wait_ge(bn_ready, 3 * b + 7)
                        dve.wait_ge(rstd_ready, b + 1)
                    dve.wait_ge(exp_ready, 2 * s + 2)
                    _wait(dve, norm0_ready, s - 1)
                    dve.reciprocal(rinv[:, h % 2, :], rsum[:, h % 2, :]).then_inc(rinv_ready, 1)
                    if h == 0 and _live(b + 1, BATCH):
                        aggregate(b + 1)
                    dve.wait_ge(rinv_ready, s + 1)
                    dve.tensor_scalar(prob[:, h % 2, 1, 0:KEYS], prob[:, h % 2, 1, 0:KEYS], rinv[:, h % 2, 1:2], None,
                                      ALU.mult).then_inc(norm1_ready, 1)
                if _live(s - 1, STEPS):
                    dve.wait_ge(pthi_ready, s)
                    dve.tensor_tensor(pt_lo[:, (h - 1) % 2, :], ps_t[:, 0:3 * TOK], pt_hi[:, (h - 1) % 2, :].bitcast(F32),
                                      ALU.subtract).then_inc(ptlo_ready, 1)
                if _live(s + 1, STEPS):
                    qk_lo(s + 1, (h + 1) % 2, (h + 1) % HEADS)
                if _live(s, STEPS):
                    if h == 6 and _live(b + 1, BATCH):
                        tokens_lo(b + 1)
                    for g in VG_AT.get(h, ()):
                        half, j = divmod(g, 3)
                        rows = P if j < 2 else MEDIA
                        dve.wait_ge(vhi_ready, VGROUPS * b + g + 1)
                        dve.tensor_tensor(v_lo[0:rows, half, j, :], ps_v[0:rows, :], v_hi[0:rows, half, j, :].bitcast(F32),
                                          ALU.subtract).then_inc(vlo_ready, 1)
                    if h == 3 and _live(b + 1, BATCH):
                        normalise(b + 1)
                if _live(s - 2, STEPS):
                    hh = (h - 2) % HEADS
                    dve.wait_ge(ohi_ready, s - 1)
                    dve.scalar_tensor_tensor(out=o_lo[:, h % 2, :], in0=ps_qa[:, TOK:2 * TOK],
                                             scalar=bkv[:, HEADS + hh:HEADS + hh + 1],
                                             in1=o_hi[:, h % 2, :].bitcast(F32), op0=ALU.add,
                                             op1=ALU.subtract).then_inc(olo_ready, 1)
                if h == 2 and _live(b - 1, BATCH):
                    rows = x_all[:, bass.ds(TT * (b - 1), TT), :]
                    dve.wait_ge(projected, HEADS * b)
                    dve.wait_ge(xb_ready, b)
                    dve.scalar_tensor_tensor(out=rows, in0=ps_y[:, :].rearrange("p (i d) -> p i d", i=TT),
                                             scalar=tg[:, 0:1], in1=rows, op0=ALU.mult,
                                             op1=ALU.add).then_inc(x2_ready, 1)

            dve.wait_ge(bn_ready, 1)
            statistics(0)
            dve.wait_ge(bn_ready, 4)
            aggregate(0)
            normalise(0)
            for n in range(4):
                if n == 1:
                    tokens_lo(0)
                dve.wait_ge(whi_ready, n + 1)
                dve.scalar_tensor_tensor(out=piece(w_lo, n), in0=piece(raw, n), scalar=SCALE if n == 0 else 1.0,
                                         in1=piece(w_hi, n).bitcast(F32), op0=ALU.mult,
                                         op1=ALU.subtract).then_inc(wlo_ready, 1)
                if n == 1:
                    qk_lo(0, 0, 0)
            dve.wait_ge(tg_ready, 1)
            dve.tensor_scalar(tgbo[:, :], bo[:, :], tg[:, 0:1], None, ALU.mult).then_inc(tg_ready, 1)
            for h in range(HEADS):
                step(0, h)
            with dve.Fori(1, BATCH - 1) as b:
                for h in range(HEADS):
                    step(b, h)
            for h in range(HEADS):
                step(BATCH - 1, h)
            for h in range(3):
                step(BATCH, h)

        @block.tensor
        def _(pe):
            def product(out, pairs, first=True, last=True):
                n = 0
                for s_hi, s_lo, m_hi, m_lo in pairs:
                    for a, m in ((s_hi, m_hi), (s_hi, m_lo), (s_lo, m_hi)):
                        n += 1
                        mm = pe.matmul(out, a, m, start=first and n == 1, stop=last and n == 3 * len(pairs))
                return mm

            def turn_tokens(b, c):
                pe.wait_ge(z_ready, 3 * (b + 1))
                if c == 0:
                    _wait(pe, vlo_ready, VGROUPS * b)
                else:
                    pe.wait_ge(tok_scaled, 2 * FC * b + 2)
                for i in range(TT):
                    pe.transpose(ps_v[:, i * P:(i + 1) * P], z[:, i, c * P:(c + 1) * P], ident[:, :])
                pe.transpose(ps_v[:, TOK:KEYS], z[0:MEDIA, 2, c * P:(c + 1) * P], ident[0:MEDIA, 0:MEDIA])\
                  .then_inc(tok_turned, 1)

            def project_qk(u, h, b):
                pe.wait_ge(lnlo_ready, b + 1)
                _wait(pe, qklo_ready, 2 * u)
                _wait(pe, olo_ready, u - 3)
                product(ps_qa[:, 0:TOK], [(wq(w_hi, c, h), wq(w_lo, c, h), ln_hi[:, c, 0:TOK], ln_lo[:, c, 0:TOK])
                                          for c in range(FC)]).then_inc(qk_projected, 1)
                product(ps_k[:, 0:KPAD], [(wk(w_hi, c, h), wk(w_lo, c, h), ln_hi[:, c, :], ln_lo[:, c, :])
                                          for c in range(FC)]).then_inc(qk_projected, 1)

            def project_v(b, g):
                half, j = divmod(g, 3)
                if g == 0:
                    pe.wait_ge(tok_scaled, 2 * FC * (b + 1))
                else:
                    pe.wait_ge(vlo_ready, VGROUPS * b + g)
                j0, j1 = (j * P, (j + 1) * P) if j < 2 else (TOK, KEYS)
                product(ps_v[0:j1 - j0, :], [(ln_hi[:, c, j0:j1], ln_lo[:, c, j0:j1], wv(w_hi, c, half), wv(w_lo, c, half))
                                             for c in range(FC)]).then_inc(v_projected, 1)

            def step(b, h):
                s = HEADS * b + h
                if _live(s, STEPS):
                    pe.wait_ge(qklo_ready, 2 * (s + 1))
                    for i in range(TT):
                        _wait(pe, exp_ready, 2 * s - 1 + i)
                        product(ps_s[i][:, 0:KPAD], [(q_hi[:, h % 2, i * P:(i + 1) * P], q_lo[:, h % 2, i * P:(i + 1) * P],
                                                      k_hi[:, h % 2, :], k_lo[:, h % 2, :])]).then_inc(scored, 1)
                if _live(s - 1, STEPS):
                    if isinstance(s, int) and s == 1:
                        pe.wait_ge(const_ready, 2)
                    pe.wait_ge(norm0_ready, s)
                    pe.wait_ge(norm1_ready, s)
                    _wait(pe, ptlo_ready, s - 1)
                    for j in range(3):
                        j0, j1 = (j * P, (j + 1) * P) if j < 2 else (TOK, KEYS)
                        for i in range(TT):
                            mm = pe.transpose(ps_t[0:j1 - j0, j * TOK + i * P:j * TOK + (i + 1) * P],
                                              prob[:, (h - 1) % 2, i, j0:j1], ident[:, :])
                    mm.then_inc(p_turned, 1)
                if _live(s + 1, STEPS):
                    project_qk(s + 1, (h + 1) % HEADS, b + 1 if h == HEADS - 1 else b)
                if _live(s, STEPS):
                    for g in VG_AT.get(h, ()):
                        if isinstance(b, int) and b == 0 and g == 0:
                            pe.wait_ge(wlo_ready, 3)
                        project_v(b, g)
                    if h in (4, 5) and _live(b + 1, BATCH):
                        turn_tokens(b + 1, h - 4)
                if _live(s - 2, STEPS):
                    hh = (h - 2) % HEADS
                    bw = b if h >= 2 else b - 1
                    half, col = hh // 4, (hh % 4) * DH
                    pe.wait_ge(ptlo_ready, s - 1)
                    pe.wait_ge(vlo_ready, VGROUPS * bw + 3 * (half + 1))
                    if _live(s + 1, STEPS):
                        pe.wait_ge(qklo_ready, 2 * (s + 1) + 1)
                    _wait(pe, olo_ready, s - 2)
                    product(ps_qa[:, TOK:2 * TOK], [
                        (v_hi[0:r, half, j, col:col + DH], v_lo[0:r, half, j, col:col + DH],
                         pt_hi[0:r, h % 2, j * TOK:(j + 1) * TOK], pt_lo[0:r, h % 2, j * TOK:(j + 1) * TOK])
                        for j, r in enumerate((P, P, MEDIA))]).then_inc(attended, 1)
                if _live(s - 3, STEPS):
                    hh = (h - 3) % HEADS
                    par = (h - 3) % 2
                    if isinstance(s, int) and s == 3:
                        pe.wait_ge(wlo_ready, 4)
                    pe.wait_ge(olo_ready, s - 2)
                    if hh == 0:
                        _wait(pe, x2_ready, b)
                    for i in range(TT):
                        for n, (a, m) in enumerate(((o_hi, w_hi), (o_hi, w_lo), (o_lo, w_hi))):
                            mm = pe.matmul(ps_y[:, i * DIM:(i + 1) * DIM], a[:, par, i * P:(i + 1) * P], wo(m, hh),
                                           start=hh == 0 and i == 0 and n == 0, stop=hh == HEADS - 1 and n == 2,
                                           skip_group_check=True)
                    mm.then_inc(projected, 1)

            pe.wait_ge(id_ready, 2)
            for c in range(FC):
                turn_tokens(0, c)
            pe.wait_ge(wlo_ready, 2)
            project_qk(0, 0, 0)
            for h in range(HEADS):
                step(0, h)
            with pe.Fori(1, BATCH - 1) as b:
                for h in range(HEADS):
                    step(b, h)
            for h in range(HEADS):
                step(BATCH - 1, h)
            for h in range(3):
                step(BATCH, h)


def ffn(nc, t, x_all, ident, raw_gu, raw_down, raw_in):
    with ExitStack() as ctx:
        def sb(name, shape, dt=F32):
            return ctx.enter_context(nc.sbuf_tensor(name, shape, dt))

        def ps(name, shape):
            return ctx.enter_context(nc.psum_tensor(name, shape, F32))

        def sem(name):
            return ctx.enter_context(nc.semaphore(name))

        gu_hi = sb("gu_hi", [P, FC, GU], F32R)
        gu_lo = sb("gu_lo", [P, FC, GU], F32R)
        dn_hi = sb("dn_hi", [P, EXP + 1, DIM], F32R)
        dn_lo = sb("dn_lo", [P, EXP + 1, DIM], F32R)
        gf = sb("gf", [P, 1])
        tgf = sb("tgf", [P, 1])
        bias = sb("bias", [P, EXP])
        before = sb("before", [P, EXP, EXP])
        mhalf2 = sb("mhalf2", [P, TT])
        eps2 = sb("eps2", [P, TT])
        stats2 = sb("stats2", [P, TT, 6])
        mv2 = sb("mv2", [P, TT, 2])
        rstd = sb("rstd", [P, 2, TT])
        z2 = sb("z2", [P, TT, DIM])
        xt_hi = sb("xt_hi", [P, 2, FC, TOK], F32R)
        xt_lo = sb("xt_lo", [P, 2, FC, TOK], F32R)
        th = sb("th", [P, 2, 512])
        act_a = sb("act_a", [P, 2, 512])
        act_h = sb("act_h", [P, TT, (EXP + 1) * I])
        act_f = sb("act_f", [P, TT, (EXP + 1) * I])
        ft_hi = sb("ft_hi", [P, 2, 512], F32R)
        ft_lo = sb("ft_lo", [P, 2, 512], F32R)
        tl = sb("tl", [P, TT, EXP])
        comb = sb("comb", [P, TT, EXP + 1])
        sig = sb("sig", [P, TT, EXP])
        choice = sb("choice", [P, 2 * TT, 4])
        hl = sb("hl", [P, 2, 2 * TT, 2])
        top = sb("top", [P, 5, 2 * TT])
        pick = sb("pick", [P, 2 * TT])
        cmp_gt = sb("cmp_gt", [P, TT * EXP, EXP])
        cmp_eq = sb("cmp_eq", [P, TT * EXP, EXP])
        rank = sb("rank", [P, TT * EXP])
        wsum = sb("wsum", [P, 3, TT])
        y_out = sb("y_out", [P, 2, DIM])

        ps_g = [ps("ps_g0", [P, 512]), ps("ps_g1", [P, 512])]
        ps_u = [ps("ps_u0", [P, 512]), ps("ps_u1", [P, 512])]
        ps_sh = ps("ps_sh", [P, 512])
        ps_x = ps("ps_x", [P, 512])
        ps_f = ps("ps_f", [P, 512])
        ps_o = ps("ps_o", [P, 512])

        vec_in, ffn_gate, wsplit_hi, wsplit_lo = sem("f_vec_in"), sem("f_gate"), sem("f_wsplit_hi"), sem("f_wsplit_lo")
        masks, half2 = sem("f_masks"), sem("f_half")
        bn2, var_ready, rstep, rstd_ready, z_ready = sem("f_bn"), sem("f_var"), sem("f_rstep"), sem("f_rstd"), sem("f_z")
        x_turned, xthi_ready, xtlo_ready = sem("f_x_turned"), sem("f_xthi"), sem("f_xtlo")
        gu_done = sem("f_gu_done")
        tanh_done, a_done, h_done = sem("f_tanh"), sem("f_a"), sem("f_h")
        logit_tanh, comb_ready, route = sem("f_logit_tanh"), sem("f_comb"), sem("f_route")
        f_ready, f_turned, fthi_ready, ftlo_ready = sem("f_f"), sem("f_turned"), sem("f_fthi"), sem("f_ftlo")
        down_done, y_ready, y_stored = sem("f_down"), sem("f_y"), [sem("f_y_stored0"), sem("f_y_stored1")]

        SLOTS = ((0, 2), (0, 0), (1, 2), (0, 1), (1, 0), (1, 1))
        BANK = {(0, 0): 0, (0, 1): 1, (1, 0): 0, (1, 1): 1}
        DOWN = ((0, 0), (0, 1), (0, 2), (1, 0), (1, 1), (1, 2))
        NU = len(SLOTS)
        WEIGHTED = ((0, 2), (0, 0), (1, 2), (0, 1), (1, 0), (1, 1))
        W0 = 0
        GC = (0, 1024, 2048)
        ROUTE_STEPS = 21

        block = ctx.enter_context(nc.Block())

        @block.sync
        def _(sp):
            sp.dma_start(gf[:, :], t["g_ffn"].unsqueeze(0).to_broadcast([P, 1])).then_inc(vec_in, 16)
            sp.dma_start(bias[:, :], t["L0_ffn_correction_bias"].unsqueeze(0).to_broadcast([P, EXP])).then_inc(vec_in, 16)
            out = t["out"].rearrange("b (i p) d -> b i p d", p=P)

            def store(p):
                for i in range(TT):
                    sp.wait_ge(y_ready, TT * p + i + 1)
                    sp.dma_start(out[bass.ds(p, 1), i].rearrange("o p d -> (o p) d"), y_out[:, i, :]).then_inc(y_stored[i], 16)

            with sp.Fori(0, PAIRS) as p:
                store(p)
            for i in range(TT):
                sp.wait_ge(y_stored[i], 16 * PAIRS)

        @block.gpsimd
        def _(pool):
            pool.memset(mhalf2[:, :], -0.5).then_inc(half2, 1)
            pool.memset(eps2[:, :], EPS).then_inc(half2, 1)
            pool.memset(before[:, :, :], 1.0).then_inc(masks, 1)
            pool.memset(comb[:, :, EXP:EXP + 1], 0.5).then_inc(masks, 1)
            pool.wait_ge(masks, 2)
            pool.affine_select(out=before[:, :, :], in_=before[:, :, :], compare_op=ALU.is_gt, fill=0.0, base=0,
                               pattern=[[1, EXP], [-1, EXP]], channel_multiplier=0).then_inc(masks, 1)

            def reciprocal_deviation(p):
                pool.wait_ge(var_ready, TT * (p + 1))
                _wait(pool, z_ready, TT * p)
                pool.wait_ge(half2, 2)
                pool.tensor_tensor(rstd[:, 0, :], mv2[:, :, 1], eps2[:, :], ALU.add).then_inc(rstep, 1)
                pool.wait_ge(rstep, p + 1)
                pool.tensor_tensor(rstd[:, 1, :], rstd[:, 0, :], mhalf2[:, :], ALU.pow).then_inc(rstd_ready, 1)

            def pair(p, par):
                for n, (i, u) in enumerate(WEIGHTED):
                    pool.wait_ge(h_done, NU * p + n + 1)
                    if n == 0:
                        pool.wait_ge(comb_ready, p + 1)
                        pool.wait_ge(masks, 3)
                    _wait(pool, f_turned, NU * (p - 1) + DOWN.index((i, u)) + 1)
                    e0, ne = UE[u], UN[u]
                    pool.tensor_tensor(act_f[:, i, e0 * I:(e0 + ne) * I].rearrange("p (e i) -> p e i", e=ne),
                                       act_h[:, i, e0 * I:(e0 + ne) * I].rearrange("p (e i) -> p e i", e=ne),
                                       comb[:, i, e0:e0 + ne].unsqueeze(2).to_broadcast([P, ne, I]),
                                       ALU.mult).then_inc(f_ready, 1)
                    if n == 1 and _live(p + 1, PAIRS):
                        reciprocal_deviation(p + 1)

            reciprocal_deviation(0)
            pair(0, 0)
            pair(1, 1)
            with pool.Fori(2, PAIRS - 2, 2) as p:
                pair(p, 0)
                pair(p + 1, 1)
            pair(PAIRS - 2, 0)
            pair(PAIRS - 1, 1)

        def place(p, n):
            return NU * p + n

        @block.scalar
        def _(act):
            act.wait_ge(vec_in, 32)
            act.activation(tgf[:, :], gf[:, :], ACT.Tanh).then_inc(ffn_gate, 1)

            def tokens_hi(p, par):
                act.wait_ge(x_turned, p + 1)
                _wait(act, gu_done, NU * (p - 1))
                act.activation(xt_hi[:, par, :, :].rearrange("p c n -> p (c n)"), ps_x[:, :], ACT.Copy).then_inc(xthi_ready, 1)

            def down_hi(p, n):
                d = place(p, n)
                w = UN[DOWN[n][1]] * I
                act.wait_ge(f_turned, d + 1)
                _wait(act, down_done, d - 1)
                act.activation(ft_hi[:, n % 2, 0:w], ps_f[:, 0:w], ACT.Copy).then_inc(fthi_ready, 1)

            def pair(p, par):
                for n, (i, u) in enumerate(SLOTS):
                    w = UN[u] * I
                    act.wait_ge(gu_done, NU * p + n + 1)
                    _wait(act, a_done, NU * p + n - 1)
                    src = ps_sh if u == 2 else ps_g[BANK[i, u]]
                    act.activation(th[:, n % 2, 0:w], src[:, 0:w], ACT.Tanh, scale=0.5).then_inc(tanh_done, 1)
                    if u == 2:
                        _wait(act, comb_ready, p)
                        act.activation(tl[:, i, :], ps_sh[:, 2 * I:2 * I + EXP], ACT.Tanh, scale=0.5).then_inc(logit_tanh, 1)
                    if _live(p - 1, PAIRS):
                        down_hi(p - 1, n)
                    if n == 4 and _live(p + 1, PAIRS):
                        tokens_hi(p + 1, 1 - par)

            tokens_hi(0, 0)
            act.wait_ge(raw_in, 16 * RAW_DMAS)
            for c0, c1 in ((2048, GU), (0, 1024), (1024, 2048)):
                act.activation(gu_hi[:, :, c0:c1], raw_gu[:, :, c0:c1], ACT.Copy).then_inc(wsplit_hi, 1)
            act.activation(dn_hi[:, :, :], raw_down[:, :, :], ACT.Copy).then_inc(wsplit_hi, 1)
            pair(0, 0)
            pair(1, 1)
            with act.Fori(2, PAIRS - 2, 2) as p:
                pair(p, 0)
                pair(p + 1, 1)
            pair(PAIRS - 2, 0)
            pair(PAIRS - 1, 1)
            for n in range(NU):
                down_hi(PAIRS - 1, n)

        @block.vector
        def _(dve):
            def statistics(p):
                for i in range(TT):
                    dve.bn_stats(stats2[:, i, :], x_all[:, bass.ds(TT * p + i, 1), :].rearrange("p o d -> p (o d)"))\
                       .then_inc(bn2, 1)

            def aggregate(p):
                for i in range(TT):
                    dve.bn_aggr(mv2[:, i, :], stats2[:, i, :]).then_inc(var_ready, 1)

            def normalise(p):
                dve.wait_ge(rstd_ready, p + 1)
                _wait(dve, x_turned, p)
                for i in range(TT):
                    dve.tensor_scalar(z2[:, i, :], x_all[:, bass.ds(TT * p + i, 1), :].rearrange("p o d -> p (o d)"),
                                      mv2[:, i, 0:1], rstd[:, 1, i:i + 1], ALU.subtract, ALU.mult).then_inc(z_ready, 1)

            def tokens_lo(p, par):
                dve.wait_ge(xthi_ready, p + 1)
                dve.tensor_tensor(xt_lo[:, par, :, :].rearrange("p c n -> p (c n)"), ps_x[:, :],
                                  xt_hi[:, par, :, :].rearrange("p c n -> p (c n)").bitcast(F32),
                                  ALU.subtract).then_inc(xtlo_ready, 1)

            def down_lo(p, n):
                d = place(p, n)
                w = UN[DOWN[n][1]] * I
                dve.wait_ge(fthi_ready, d + 1)
                dve.tensor_tensor(ft_lo[:, n % 2, 0:w], ps_f[:, 0:w], ft_hi[:, n % 2, 0:w].bitcast(F32),
                                  ALU.subtract).then_inc(ftlo_ready, 1)

            def output(p, i):
                dve.wait_ge(down_done, place(p, 3 * i + 3))
                _wait(dve, y_stored[i], 16 * p)
                if isinstance(p, int) and p == 0:
                    dve.wait_ge(ffn_gate, 1)
                dve.scalar_tensor_tensor(out=y_out[:, i, :], in0=ps_o[:, 0:DIM], scalar=tgf[:, 0:1],
                                         in1=x_all[:, bass.ds(TT * p + i, 1), :].rearrange("p o d -> p (o d)"),
                                         op0=ALU.mult, op1=ALU.add).then_inc(y_ready, 1)

            def routing(p):
                dve.wait_ge(logit_tanh, TT * (p + 1))
                _wait(dve, f_ready, NU * p)
                if isinstance(p, int) and p == 0:
                    dve.wait_ge(masks, 3)
                    dve.wait_ge(vec_in, 32)
                done = 0

                def link(ins):
                    nonlocal done
                    done += 1
                    ins.then_inc(route, 1)
                    dve.wait_ge(route, ROUTE_STEPS * p + done)

                flat = choice[:, :, :].rearrange("p a b -> p (a b)")
                by_tile = flat.rearrange("p (i e) -> p i e", i=TT)
                link(dve.tensor_scalar(sig[:, :, :], tl[:, :, :], 0.5, 0.5, ALU.mult, ALU.add))
                link(dve.tensor_tensor(by_tile, sig[:, :, :], bias[:, :].unsqueeze(1).to_broadcast([P, TT, EXP]), ALU.add))
                link(dve.tensor_tensor(hl[:, 0], choice[:, :, 0:2], choice[:, :, 2:4], ALU.max))
                link(dve.tensor_tensor(hl[:, 1], choice[:, :, 0:2], choice[:, :, 2:4], ALU.min))
                link(dve.tensor_tensor(top[:, 0], hl[:, 0, :, 0], hl[:, 0, :, 1], ALU.max))
                link(dve.tensor_tensor(top[:, 1], hl[:, 0, :, 0], hl[:, 0, :, 1], ALU.min))
                link(dve.tensor_tensor(top[:, 2], hl[:, 1, :, 0], hl[:, 1, :, 1], ALU.max))
                link(dve.tensor_tensor(top[:, 3], top[:, 1], top[:, 2], ALU.max))
                link(dve.tensor_tensor(top[:, 4], top[:, 0], top[:, 3], ALU.add))
                sums = top[:, 4].rearrange("p (i g) -> p i g", g=2)
                picks = pick[:, :].rearrange("p (i g) -> p i g", g=2)
                link(dve.tensor_tensor(picks[:, :, 0], sums[:, :, 0], sums[:, :, 1], ALU.is_ge))
                link(dve.tensor_tensor(picks[:, :, 1], sums[:, :, 1], sums[:, :, 0], ALU.is_gt))
                link(dve.tensor_tensor(choice[:, :, :], choice[:, :, :], pick[:, :].unsqueeze(2).to_broadcast([P, 2 * TT, 4]), ALU.mult))
                other = by_tile.unsqueeze(2).to_broadcast([P, TT, EXP, EXP])
                own = by_tile.unsqueeze(3).to_broadcast([P, TT, EXP, EXP])
                gt4 = cmp_gt[:, :, :].rearrange("p (i e) f -> p i e f", i=TT)
                eq4 = cmp_eq[:, :, :].rearrange("p (i e) f -> p i e f", i=TT)
                link(dve.tensor_tensor(gt4, other, own, ALU.is_gt))
                link(dve.tensor_tensor(eq4, other, own, ALU.is_equal))
                link(dve.tensor_tensor(eq4, eq4, before[:, :, :].unsqueeze(1).to_broadcast([P, TT, EXP, EXP]), ALU.mult))
                link(dve.tensor_tensor(cmp_gt[:, :, :], cmp_gt[:, :, :], cmp_eq[:, :, :], ALU.add))
                link(dve.tensor_reduce(rank[:, :], cmp_gt[:, :, :], AX.X, ALU.add))
                link(dve.scalar_tensor_tensor(out=sig[:, :, :], in0=rank[:, :].rearrange("p (i e) -> p i e", i=TT), scalar=2.0,
                                              in1=sig[:, :, :], op0=ALU.is_lt, op1=ALU.mult))
                link(dve.tensor_reduce(wsum[:, 0, :], sig[:, :, :], AX.X, ALU.add))
                link(dve.tensor_scalar(wsum[:, 1, :], wsum[:, 0, :], 1e-20, None, ALU.add))
                link(dve.reciprocal(wsum[:, 2, :], wsum[:, 1, :]))
                assert done == ROUTE_STEPS
                dve.scalar_tensor_tensor(out=comb[:, :, 0:EXP], in0=sig[:, :, :], scalar=0.5,
                                         in1=wsum[:, 2, :].unsqueeze(2).to_broadcast([P, TT, EXP]),
                                         op0=ALU.mult, op1=ALU.mult).then_inc(comb_ready, 1)

            def pair(p, par):
                for n, (i, u) in enumerate(SLOTS):
                    w, e0 = UN[u] * I, UE[u]
                    if n == 1 and _live(p + 1, PAIRS):
                        dve.wait_ge(bn2, TT * (p + 2))
                        dve.wait_ge(rstd_ready, p + 1)
                    g_bank = ps_sh[:, 0:w] if u == 2 else ps_g[BANK[i, u]][:, 0:w]
                    u_bank = ps_sh[:, w:2 * w] if u == 2 else ps_u[BANK[i, u]][:, 0:w]
                    dve.wait_ge(tanh_done, NU * p + n + 1)
                    if u == 2:
                        dve.wait_ge(logit_tanh, TT * p + i + 1)
                    _wait(dve, h_done, NU * p + n - 1)
                    dve.scalar_tensor_tensor(out=act_a[:, n % 2, 0:w], in0=th[:, n % 2, 0:w], scalar=1.0, in1=g_bank,
                                             op0=ALU.add, op1=ALU.mult).then_inc(a_done, 1)
                    if n == 1 and _live(p + 1, PAIRS):
                        aggregate(p + 1)
                    dve.wait_ge(a_done, NU * p + n + 1)
                    _wait(dve, f_ready, NU * (p - 1) + n + 1)
                    dve.tensor_tensor(act_h[:, i, e0 * I:e0 * I + w], act_a[:, n % 2, 0:w], u_bank,
                                      ALU.mult).then_inc(h_done, 1)
                    if _live(p - 1, PAIRS):
                        down_lo(p - 1, n)
                        if n == 3:
                            output(p - 1, 0)
                    if n == 0:
                        if _live(p - 2, PAIRS):
                            output(p - 2, 1)
                        if _live(p + 1, PAIRS):
                            statistics(p + 1)
                    if n == 2:
                        routing(p)
                        if _live(p + 1, PAIRS):
                            normalise(p + 1)
                    if n == 4 and _live(p + 1, PAIRS):
                        tokens_lo(p + 1, 1 - par)

            statistics(0)
            dve.wait_ge(bn2, TT)
            aggregate(0)
            normalise(0)
            tokens_lo(0, 0)
            for n, (c0, c1) in enumerate(((2048, GU), (0, 1024), (1024, 2048))):
                dve.wait_ge(wsplit_hi, n + 1)
                dve.tensor_tensor(gu_lo[:, :, c0:c1], raw_gu[:, :, c0:c1], gu_hi[:, :, c0:c1].bitcast(F32),
                                  ALU.subtract).then_inc(wsplit_lo, 1)
            dve.wait_ge(wsplit_hi, 4)
            dve.tensor_tensor(dn_lo[:, :, :], raw_down[:, :, :], dn_hi[:, :, :].bitcast(F32),
                              ALU.subtract).then_inc(wsplit_lo, 1)
            pair(0, 0)
            pair(1, 1)
            with dve.Fori(2, PAIRS - 2, 2) as p:
                pair(p, 0)
                pair(p + 1, 1)
            pair(PAIRS - 2, 0)
            pair(PAIRS - 1, 1)
            output(PAIRS - 2, 1)
            for n in range(NU):
                down_lo(PAIRS - 1, n)
                if n == 3:
                    output(PAIRS - 1, 0)
            output(PAIRS - 1, 1)

        @block.tensor
        def _(pe):
            def turn_tokens(p):
                pe.wait_ge(z_ready, TT * (p + 1))
                _wait(pe, xtlo_ready, p)
                for c in range(FC):
                    for i in range(TT):
                        mm = pe.transpose(ps_x[:, c * TOK + i * P:c * TOK + (i + 1) * P], z2[:, i, c * P:(c + 1) * P], ident[:, :])
                mm.then_inc(x_turned, 1)

            def gate_up(p, par, n):
                i, u = SLOTS[n]
                tok = slice(i * P, (i + 1) * P)
                last = {0: NU * (p - 1) + 3, 1: NU * (p - 1) + 5, 2: NU * p + 1, 3: NU * (p - 1) + 6,
                        4: NU * p + 2, 5: NU * p + 4}[n]
                _wait(pe, h_done, last)
                if n == 0:
                    pe.wait_ge(xtlo_ready, p + 1)
                w = 2 * I + EXP if u == 2 else 512
                banks = [(ps_sh, GC[2])] if u == 2 else [(ps_g[BANK[i, u]], GC[u]), (ps_u[BANK[i, u]], GC[u] + 512)]
                for bank, c0 in banks:
                    k = 0
                    for c in range(FC):
                        for a, m in ((xt_hi, gu_hi), (xt_hi, gu_lo), (xt_lo, gu_hi)):
                            mm = pe.matmul(bank[:, 0:w], a[:, par, c, tok], m[:, c, c0:c0 + w], start=k == 0, stop=k == 5)
                            k += 1
                mm.then_inc(gu_done, 1)

            def turn_f(p, n):
                i, u = DOWN[n]
                d = place(p, n)
                pe.wait_ge(f_ready, NU * p + WEIGHTED.index((i, u)) + 1)
                _wait(pe, ftlo_ready, d)
                for k in range(UN[u]):
                    e = UE[u] + k
                    mm = pe.transpose(ps_f[:, k * P:(k + 1) * P], act_f[:, i, e * I:(e + 1) * I], ident[:, :])
                mm.then_inc(f_turned, 1)

            def down(p, n):
                i, u = DOWN[n]
                pe.wait_ge(ftlo_ready, place(p, n) + 1)
                if u == 0:
                    _wait(pe, y_ready, TT * p + i)
                for k in range(UN[u]):
                    e = UE[u] + k
                    for m, (a, wd) in enumerate(((ft_hi, dn_hi), (ft_hi, dn_lo), (ft_lo, dn_hi))):
                        mm = pe.matmul(ps_o[:, 0:DIM], a[:, n % 2, k * P:(k + 1) * P], wd[:, e, :],
                                       start=u == 0 and k == 0 and m == 0, stop=u == 2 and m == 2)
                mm.then_inc(down_done, 1)

            def pair(p, par):
                for n in range(NU):
                    if isinstance(p, int) and p == 0 and n in (0, 1, 3):
                        pe.wait_ge(wsplit_lo, {0: 1, 1: 2, 3: 3}[n])
                    gate_up(p, par, n)
                    if n == 0:
                        if _live(p - 2, PAIRS):
                            down(p - 2, NU - 1)
                    elif _live(p - 1, PAIRS):
                        if isinstance(p, int) and p == 1 and n == 1:
                            pe.wait_ge(wsplit_lo, 4)
                        down(p - 1, n - 1)
                    if n == 4 and _live(p + 1, PAIRS):
                        turn_tokens(p + 1)
                    if _live(p - 1, PAIRS):
                        turn_f(p - 1, n)

            turn_tokens(0)
            pair(0, 0)
            pair(1, 1)
            with pe.Fori(2, PAIRS - 2, 2) as p:
                pair(p, 0)
                pair(p + 1, 1)
            pair(PAIRS - 2, 0)
            pair(PAIRS - 1, 1)
            down(PAIRS - 2, NU - 1)
            for n in range(NU):
                if n:
                    down(PAIRS - 1, n - 1)
                turn_f(PAIRS - 1, n)
            down(PAIRS - 1, NU - 1)


def load_ffn_weights(engine, t, raw_gu, raw_down, raw_in):
    for c in range(FC):
        rows = slice(c * P, (c + 1) * P)
        for half in range(2):
            for k, name in enumerate(("w_gate", "w_up")):
                engine.dma_start(raw_gu[:, c, half * 1024 + k * 512:half * 1024 + (k + 1) * 512].rearrange("p (e i) -> p e i", e=4),
                                 t["L0_ffn_" + name][half * 4:half * 4 + 4, rows, :].rearrange("e p i -> p e i")).then_inc(raw_in, 16)
    for k, name in enumerate(("sw_gate", "sw_up")):
        engine.dma_start(raw_gu[:, :, 2048 + k * I:2048 + (k + 1) * I],
                         t["L0_ffn_" + name].rearrange("(c p) i -> p c i", p=P)).then_inc(raw_in, 16)
    engine.dma_start(raw_down[:, 0:EXP, :], t["L0_ffn_w_down"].rearrange("e p d -> p e d")).then_inc(raw_in, 16)
    engine.dma_start(raw_down[:, EXP, :], t["L0_ffn_sw_down"]).then_inc(raw_in, 16)
    for c in range(FC):
        engine.dma_start(raw_gu[:, c, 2048 + 2 * I:GU],
                         t["L0_ffn_router_weight"][:, c * P:(c + 1) * P].rearrange("e p -> p e"),
                         allow_slow_non_contiguous=True).then_inc(raw_in, 16)


def build(nc, t):
    with ExitStack() as ctx:
        x_all = ctx.enter_context(nc.sbuf_tensor("x_all", [P, TT * BATCH, DIM], F32))
        ident = ctx.enter_context(nc.sbuf_tensor("ident", [P, P], F32))
        raw = ctx.enter_context(nc.sbuf_tensor("raw", [P, RAW], F32))
        raw_in = ctx.enter_context(nc.semaphore("raw_in"))
        raw_gu = raw[:, 0:FC * GU].rearrange("p (c n) -> p c n", c=FC)
        raw_down = raw[:, FC * GU:FC * GU + (EXP + 1) * DIM].rearrange("p (e d) -> p e d", e=EXP + 1)
        attention(nc, t, x_all, ident, raw, lambda engine: load_ffn_weights(engine, t, raw_gu, raw_down, raw_in))
        ffn(nc, t, x_all, ident, raw_gu, raw_down, raw_in)


_INS = ['x', 'ctx_1024', 'g_xattn', 'g_ffn', 'L0_xattn_gamma_media', 'L0_xattn_beta_media', 'L0_xattn_gamma_lat',
        'L0_xattn_beta_lat', 'L0_xattn_Wq', 'L0_xattn_bq', 'L0_xattn_Wkv', 'L0_xattn_bkv', 'L0_xattn_Wo', 'L0_xattn_bo',
        'L0_ffn_router_weight', 'L0_ffn_correction_bias', 'L0_ffn_w_gate', 'L0_ffn_w_up', 'L0_ffn_w_down',
        'L0_ffn_sw_gate', 'L0_ffn_sw_up', 'L0_ffn_sw_down']


def kernel(**inputs):
    import numpy as _np
    import concourse.bacc as _bacc
    from concourse import mybir as _mybir
    from concourse.bass_utils import run_bass_kernel_spmd as _run

    nc = _bacc.Bacc("TRN2", target_bir_lowering=False, num_devices=1)
    arrays, t = {}, {}
    for name in _INS:
        a = _np.ascontiguousarray(inputs[name])
        arrays[f"in_{name}_dram"] = a
        t[name] = nc.dram_tensor(f"in_{name}_dram", a.shape, _mybir.dt.from_np(a.dtype), kind="ExternalInput").ap()
    t["out"] = nc.dram_tensor("out_0_dram", (BATCH, TOK, DIM), F32, kind="ExternalOutput").ap()
    build(nc, t)
    r = _run(nc, [arrays], core_ids=[0])
    return r.results[0]["out_0_dram"]
```

```python
from contextlib import ExitStack

import concourse.bass as bass
from concourse import mybir

F32 = mybir.dt.float32
F32R = mybir.dt.float32r
ALU = mybir.AluOpType
ACT = mybir.ActivationFunctionType
AX = mybir.AxisListType

P = 128
EPS = 1e-5
BATCH, TOK, DIM = 16, 256, 256
MEDIA = 77
HEADS, DH = 8, 128
INNER = HEADS * DH
KEYS = TOK + MEDIA
KPAD = KEYS + 1
FC = DIM // P
TT = TOK // P
STEPS = BATCH * HEADS
VGROUPS = 6
VG_AT = {7: 0, 0: 1, 1: 2, 2: 3, 3: 4, 4: 5}
SCALE = float(DH) ** -0.5

EXP, I = 8, 128
UNITS = 3
UN = (4, 4, 1)
UE = (0, 4, 8)
RAW = 3 * FC * INNER + HEADS * DIM
GU = 2 * (EXP + 1) * I + EXP
RAW_DMAS = 14
PAIRS = BATCH


def _wait(engine, sem, n):
    if not isinstance(n, int) or n > 0:
        engine.wait_ge(sem, n)


def _live(n, end):
    return not isinstance(n, int) or 0 <= n < end


def attention(nc, t, x_all, ident, raw, load_ffn):
    with ExitStack() as ctx:
        def sb(name, shape, dt=F32):
            return ctx.enter_context(nc.sbuf_tensor(name, shape, dt))

        def ps(name, shape):
            return ctx.enter_context(nc.psum_tensor(name, shape, F32))

        def sem(name):
            return ctx.enter_context(nc.semaphore(name))

        QO, KVO, OO = 0, FC * INNER, 3 * FC * INNER
        WN = OO + HEADS * DIM
        w_hi = sb("w_hi", [P, WN], F32R)
        w_lo = sb("w_lo", [P, WN], F32R)
        def piece(w, n):
            if n == 0:
                return w[:, QO:KVO].rearrange("p (c n) -> p c n", c=FC)
            if n == 3:
                return w[:, OO:WN].rearrange("p (c n) -> p c n", c=HEADS)
            return w[:, KVO:OO].rearrange("p (c n) -> p c n", c=FC)[:, :, (n - 1) * INNER:n * INNER]

        def wq(w, c, h):
            return piece(w, 0)[:, c, h * DH:(h + 1) * DH]

        def wk(w, c, h):
            return piece(w, 1)[:, c, h * DH:(h + 1) * DH]

        def wv(w, c, half):
            return piece(w, 2)[:, c, half * 512:(half + 1) * 512]

        def wo(w, h):
            return piece(w, 3)[:, h, :]

        VR = 4 * FC + 3 * HEADS
        vec_rows = sb("vec_rows", [VR, P])
        vecs = sb("vecs", [P, VR])
        gb = vecs[:, 0:4 * FC].rearrange("p (n c) -> p n c", n=4)
        bkv = vecs[:, 4 * FC + HEADS:VR]
        bqs = sb("bqs", [P, HEADS])
        bo = sb("bo", [P, DIM])
        tgbo = sb("tgbo", [P, DIM])
        gx = sb("gx", [P, 1])
        tg = sb("tg", [P, 1])
        ctx_in = sb("ctx_in", [MEDIA, DIM])
        stats = sb("stats", [P, 3, 6])
        mv = sb("mv", [P, 3, 2])
        rs = sb("rs", [P, 5, 3])
        mhalf = sb("mhalf", [P, 3])
        eps3 = sb("eps3", [P, 3])
        z = sb("z", [P, 3, DIM])
        lnf = sb("lnf", [P, FC, KPAD])
        ln_hi = sb("ln_hi", [P, FC, KPAD], F32R)
        ln_lo = sb("ln_lo", [P, FC, KPAD], F32R)
        q_hi = sb("q_hi", [P, 2, TOK], F32R)
        q_lo = sb("q_lo", [P, 2, TOK], F32R)
        k_hi = sb("k_hi", [P, 2, KPAD], F32R)
        k_lo = sb("k_lo", [P, 2, KPAD], F32R)
        v_hi = sb("v_hi", [P, 2, 3, 512], F32R)
        v_lo = sb("v_lo", [P, 2, 3, 512], F32R)
        prob = sb("prob", [P, 2, TT, KPAD])
        nmax = sb("nmax", [P, 2, TT])
        rsum = sb("rsum", [P, 2, TT])
        rinv = sb("rinv", [P, 2, TT])
        pt_hi = sb("pt_hi", [P, 2, 3 * TOK], F32R)
        pt_lo = sb("pt_lo", [P, 2, 3 * TOK], F32R)
        o_hi = sb("o_hi", [P, 2, TOK], F32R)
        o_lo = sb("o_lo", [P, 2, TOK], F32R)

        ps_s = [ps("ps_s0", [P, 512]), ps("ps_s1", [P, 512])]
        ps_qa = ps("ps_qa", [P, 512])
        ps_k = ps("ps_k", [P, 512])
        ps_v = ps("ps_v", [P, 512])
        ps_t = ps("ps_t", [P, 1024])
        ps_y = ps("ps_y", [P, 512])

        x_in = [sem("x_in0"), sem("x_in1"), sem("x_in2")]
        vec_in, media_in = sem("vec_in"), sem("media_in")
        rows_in, rows_turned = sem("rows_in"), sem("rows_turned")
        w_in = [sem(f"w_in{n}") for n in range(4)]
        id_ready, const_ready, tg_ready = sem("id_ready"), sem("const_ready"), sem("tg_ready")
        bias_ready, half_ready = sem("bias_ready"), sem("half_ready")
        whi_ready, wlo_ready = sem("whi_ready"), sem("wlo_ready")
        stats_ready, rstd_ready, rstd_step, z_ready = sem("stats_ready"), sem("rstd_ready"), sem("rstd_step"), sem("z_ready")
        bn_ready = sem("bn_ready")
        tok_turned, tok_scaled, lnhi_ready, lnlo_ready = sem("tok_turned"), sem("tok_scaled"), sem("lnhi_ready"), sem("lnlo_ready")
        qk_projected, qhi_ready, khi_ready, qklo_ready = sem("qk_projected"), sem("qhi_ready"), sem("khi_ready"), sem("qklo_ready")
        v_projected, vhi_ready, vlo_ready = sem("v_projected"), sem("vhi_ready"), sem("vlo_ready")
        scored, max_ready, exp_ready, rinv_ready = sem("scored"), sem("max_ready"), sem("exp_ready"), sem("rinv_ready")
        norm0_ready, norm1_ready = sem("norm0_ready"), sem("norm1_ready")
        p_turned, pthi_ready, ptlo_ready = sem("p_turned"), sem("pthi_ready"), sem("ptlo_ready")
        attended, ohi_ready, olo_ready = sem("attended"), sem("ohi_ready"), sem("olo_ready")
        projected, xb_ready, x2_ready = sem("projected"), sem("xb_ready"), sem("x2_ready")

        block = ctx.enter_context(nc.Block())

        @block.sync
        def _(sp):
            x_tiles = t["x"].rearrange("b (i p) d -> p (b i) d", p=P)
            sp.dma_start(x_all[:, 0:TT, :], x_tiles[:, 0:TT, :]).then_inc(x_in[0], 16)
            sp.dma_start(ctx_in[:, :], t["ctx_1024"][0]).then_inc(media_in, 16)
            row = 0
            for name, rows in (("gamma_lat", FC), ("beta_lat", FC), ("gamma_media", FC), ("beta_media", FC),
                               ("bq", HEADS), ("bkv", 2 * HEADS)):
                sp.dma_start(vec_rows[row:row + rows, :],
                             t["L0_xattn_" + name].rearrange("(r p) -> r p", p=P)).then_inc(rows_in, 16)
                row += rows
            sp.dma_start(piece(raw, 0), t["L0_xattn_Wq"].rearrange("(c p) n -> p c n", p=P)).then_inc(w_in[0], 16)
            kv = t["L0_xattn_Wkv"].rearrange("(c p) n -> p c n", p=P)
            for n in (1, 2):
                sp.dma_start(piece(raw, n), kv[:, :, (n - 1) * INNER:n * INNER]).then_inc(w_in[n], 16)
            sp.dma_start(piece(raw, 3), t["L0_xattn_Wo"].rearrange("(c p) n -> p c n", p=P)).then_inc(w_in[3], 16)
            for n, (b0, b1) in enumerate(((1, 2), (2, BATCH))):
                sp.dma_start(x_all[:, TT * b0:TT * b1, :], x_tiles[:, TT * b0:TT * b1, :]).then_inc(x_in[n + 1], 16)
            sp.wait_ge(wlo_ready, 4)
            load_ffn(sp)
            with sp.Fori(1, BATCH) as b:
                sp.wait_ge(z_ready, 3 * b)
                sp.dma_start(ctx_in[:, :], t["ctx_1024"][bass.ds(b, 1)].rearrange("o j d -> (o j) d")).then_inc(media_in, 16)

        @block.gpsimd
        def _(pool):
            pool.memset(ident[:, :], 0.0).then_inc(id_ready, 1)
            pool.memset(mhalf[:, :], -0.5).then_inc(half_ready, 1)
            pool.memset(eps3[:, :], EPS).then_inc(half_ready, 1)
            pool.wait_ge(id_ready, 1)
            pool.affine_select(out=ident[:, :], in_=ident[:, :], compare_op=ALU.not_equal, fill=1.0, base=0,
                               pattern=[[-1, P]], channel_multiplier=1).then_inc(id_ready, 1)

            def reciprocal_deviations(b):
                ve, r1, sq, ve2, rr = (rs[:, n, :] for n in range(5))
                pool.wait_ge(stats_ready, 3 * (b + 1))
                _wait(pool, z_ready, 3 * b)
                pool.wait_ge(half_ready, 2)
                var = mv[:, :, 1]
                pool.tensor_tensor(ve, var, eps3[:, :], ALU.add).then_inc(rstd_step, 1)
                pool.wait_ge(rstd_step, 6 * b + 1)
                pool.tensor_tensor(r1, ve, mhalf[:, :], ALU.pow).then_inc(rstd_step, 1)
                pool.wait_ge(rstd_step, 6 * b + 2)
                pool.tensor_tensor(sq, r1, r1, ALU.mult).then_inc(rstd_step, 1)
                pool.wait_ge(rstd_step, 6 * b + 3)
                pool.tensor_tensor(sq, sq, var, ALU.mult).then_inc(rstd_step, 1)
                pool.wait_ge(rstd_step, 6 * b + 4)
                pool.tensor_tensor(ve2, sq, eps3[:, :], ALU.add).then_inc(rstd_step, 1)
                pool.wait_ge(rstd_step, 6 * b + 5)
                pool.tensor_tensor(sq, ve2, mhalf[:, :], ALU.pow).then_inc(rstd_step, 1)
                pool.wait_ge(rstd_step, 6 * b + 6)
                pool.tensor_tensor(rr, r1, sq, ALU.mult).then_inc(rstd_ready, 1)

            def step(b, h):
                s = HEADS * b + h
                pool.wait_ge(rinv_ready, s + 1)
                pool.tensor_tensor(prob[:, h % 2, 0, 0:KEYS], prob[:, h % 2, 0, 0:KEYS],
                                   rinv[:, h % 2, 0:1].to_broadcast([P, KEYS]), ALU.mult).then_inc(norm0_ready, 1)
                if h == 2 and _live(b + 1, BATCH):
                    reciprocal_deviations(b + 1)
                if h == 4:
                    rows = x_all[:, bass.ds(TT * b, TT), :]
                    pool.wait_ge(z_ready, 3 * (b + 1))
                    pool.wait_ge(tg_ready, 2)
                    pool.tensor_tensor(rows, rows, tgbo[:, :].unsqueeze(1).to_broadcast([P, TT, DIM]),
                                       ALU.add).then_inc(xb_ready, 1)

            reciprocal_deviations(0)
            for h in range(HEADS):
                step(0, h)
            with pool.Fori(1, BATCH - 1) as b:
                for h in range(HEADS):
                    step(b, h)
            for h in range(HEADS):
                step(BATCH - 1, h)

        @block.scalar
        def _(act):
            act.dma_start(gx[:, :], t["g_xattn"].unsqueeze(0).to_broadcast([P, 1])).then_inc(vec_in, 16)
            act.dma_start(bo[:, :], t["L0_xattn_bo"].unsqueeze(0).to_broadcast([P, DIM])).then_inc(vec_in, 16)
            act.wait_ge(vec_in, 32)
            act.activation(tg[:, :], gx[:, :], ACT.Tanh).then_inc(tg_ready, 1)
            act.wait_ge(rows_turned, 1)
            act.activation(vecs[:, :], ps_y[:, 0:VR], ACT.Copy).then_inc(bias_ready, 1)
            act.wait_ge(bias_ready, 1)
            act.activation(bqs[:, :], vecs[:, 4 * FC:4 * FC + HEADS], ACT.Copy, scale=SCALE).then_inc(bias_ready, 1)

            def turned_tokens(b, c):
                act.wait_ge(tok_turned, FC * b + c + 1)
                _wait(act, lnlo_ready, b)
                act.activation(lnf[:, c, 0:TOK], ps_v[:, 0:TOK], ACT.Identity, bias=gb[:, 1, c:c + 1],
                               scale=gb[:, 0, c:c + 1]).then_inc(tok_scaled, 1)
                act.activation(lnf[:, c, TOK:KEYS], ps_v[:, TOK:KEYS], ACT.Identity, bias=gb[:, 3, c:c + 1],
                               scale=gb[:, 2, c:c + 1]).then_inc(tok_scaled, 1)

            def tokens_hi(b):
                act.wait_ge(tok_scaled, 2 * FC * (b + 1))
                _wait(act, qk_projected, 2 * HEADS * b)
                _wait(act, v_projected, VGROUPS * b)
                act.activation(ln_hi[:, :, :], lnf[:, :, :], ACT.Copy).then_inc(lnhi_ready, 1)

            def k_part(u, par, h):
                act.wait_ge(qk_projected, 2 * u + 1)
                _wait(act, scored, 2 * (u - 1))
                act.activation(k_hi[:, par, :], ps_k[:, 0:KPAD], ACT.Identity,
                               bias=bkv[:, h:h + 1]).then_inc(khi_ready, 1)

            def q_part(u, par, h):
                act.wait_ge(qk_projected, 2 * u + 2)
                act.activation(q_hi[:, par, :], ps_qa[:, 0:TOK], ACT.Identity,
                               bias=bqs[:, h:h + 1]).then_inc(qhi_ready, 1)

            def v_piece(b, g):
                half, j = divmod(g, 3)
                act.wait_ge(v_projected, VGROUPS * b + g + 1)
                _wait(act, attended, HEADS * b - 4 + 4 * half)
                rows = P if j < 2 else MEDIA
                act.activation(v_hi[0:rows, half, j, :], ps_v[0:rows, :], ACT.Copy).then_inc(vhi_ready, 1)

            def exponentials(s, h, i):
                act.wait_ge(max_ready, 2 * s + i + 1)
                _wait(act, p_turned, s - 1)
                act.activation(prob[:, h % 2, i, 0:KEYS], ps_s[i][:, 0:KEYS], ACT.Exp,
                               bias=nmax[:, h % 2, i:i + 1],
                               accum_out=rsum[:, h % 2, i:i + 1]).then_inc(exp_ready, 1)

            def step(b, h):
                s = HEADS * b + h
                if _live(s - 3, STEPS):
                    hh = (h - 3) % HEADS
                    act.wait_ge(attended, s - 2)
                    _wait(act, projected, s - 4)
                    act.activation(o_hi[:, (h - 3) % 2, :], ps_qa[:, TOK:2 * TOK], ACT.Identity,
                                   bias=bkv[:, HEADS + hh:HEADS + hh + 1]).then_inc(ohi_ready, 1)
                if _live(s, STEPS):
                    if h == 6 and _live(b + 1, BATCH):
                        turned_tokens(b + 1, 1)
                    exponentials(s, h, 0)
                if _live(s + 1, STEPS):
                    k_part(s + 1, (h + 1) % 2, (h + 1) % HEADS)
                if _live(s, STEPS):
                    exponentials(s, h, 1)
                if _live(s + 1, STEPS):
                    q_part(s + 1, (h + 1) % 2, (h + 1) % HEADS)
                if h == 6 and _live(b + 1, BATCH):
                    tokens_hi(b + 1)
                if _live(s - 1, STEPS):
                    act.wait_ge(p_turned, s)
                    _wait(act, attended, s - 2)
                    act.activation(pt_hi[:, (h - 1) % 2, :], ps_t[:, 0:3 * TOK], ACT.Copy).then_inc(pthi_ready, 1)
                bv = b + 1 if h == 7 else b
                if h in VG_AT and _live(bv, BATCH):
                    v_piece(bv, VG_AT[h])
                if h == 5 and _live(b + 1, BATCH):
                    turned_tokens(b + 1, 0)

            for n in range(4):
                if n == 1:
                    act.wait_ge(const_ready, 2)
                    for c in range(FC):
                        turned_tokens(0, c)
                    tokens_hi(0)
                act.wait_ge(w_in[n], 16)
                act.activation(piece(w_hi, n), piece(raw, n), ACT.Copy,
                               scale=SCALE if n == 0 else 1.0).then_inc(whi_ready, 1)
                if n == 1:
                    act.wait_ge(bias_ready, 2)
                    act.wait_ge(qk_projected, 1)
                    k_part(0, 0, 0)
                    q_part(0, 0, 0)
            v_piece(0, 0)
            for h in range(HEADS):
                step(0, h)
            with act.Fori(1, BATCH - 1) as b:
                for h in range(HEADS):
                    step(b, h)
            for h in range(HEADS):
                step(BATCH - 1, h)
            for h in range(3):
                step(BATCH, h)

        @block.vector
        def _(dve):
            dve.memset(mv[:, :, :], 1.0).then_inc(bn_ready, 1)
            dve.memset(lnf[:, :, KEYS:KPAD], 0.0).then_inc(const_ready, 1)
            dve.memset(ps_t[:, :], 0.0).then_inc(const_ready, 1)

            def statistics(b):
                dve.wait_ge(x_in[min(b, 2) if isinstance(b, int) else 2], 16)
                for i in range(TT):
                    dve.bn_stats(stats[:, i, :], x_all[:, bass.ds(TT * b + i, 1), :].rearrange("p o d -> p (o d)"))\
                       .then_inc(bn_ready, 1)
                dve.wait_ge(media_in, 16 * (b + 1))
                dve.bn_stats(stats[0:MEDIA, 2, :], ctx_in[:, :]).then_inc(bn_ready, 1)

            def aggregate(b):
                for i in range(3):
                    rows = P if i < 2 else MEDIA
                    dve.bn_aggr(mv[0:rows, i, :], stats[0:rows, i, :]).then_inc(stats_ready, 1)

            def normalise(b):
                dve.wait_ge(rstd_ready, b + 1)
                _wait(dve, tok_turned, FC * b)
                for i in range(TT):
                    dve.tensor_scalar(z[:, i, :], x_all[:, bass.ds(TT * b + i, 1), :].rearrange("p o d -> p (o d)"),
                                      mv[:, i, 0:1], rs[:, 4, i:i + 1], ALU.subtract, ALU.mult).then_inc(z_ready, 1)
                dve.tensor_scalar(z[0:MEDIA, 2, :], ctx_in[:, :], mv[0:MEDIA, 2, 0:1], rs[0:MEDIA, 1, 2:3],
                                  ALU.subtract, ALU.mult).then_inc(z_ready, 1)

            def tokens_lo(b):
                dve.wait_ge(lnhi_ready, b + 1)
                dve.tensor_tensor(ln_lo[:, :, :], lnf[:, :, :], ln_hi[:, :, :].bitcast(F32),
                                  ALU.subtract).then_inc(lnlo_ready, 1)

            def k_part(u, par, h):
                dve.wait_ge(khi_ready, u + 1)
                dve.scalar_tensor_tensor(out=k_lo[:, par, :], in0=ps_k[:, 0:KPAD], scalar=bkv[:, h:h + 1],
                                         in1=k_hi[:, par, :].bitcast(F32), op0=ALU.add,
                                         op1=ALU.subtract).then_inc(qklo_ready, 1)

            def q_part(u, par, h):
                dve.wait_ge(qhi_ready, u + 1)
                dve.scalar_tensor_tensor(out=q_lo[:, par, :], in0=ps_qa[:, 0:TOK], scalar=bqs[:, h:h + 1],
                                         in1=q_hi[:, par, :].bitcast(F32), op0=ALU.add,
                                         op1=ALU.subtract).then_inc(qklo_ready, 1)

            def v_piece(b, g):
                half, j = divmod(g, 3)
                rows = P if j < 2 else MEDIA
                dve.wait_ge(vhi_ready, VGROUPS * b + g + 1)
                dve.tensor_tensor(v_lo[0:rows, half, j, :], ps_v[0:rows, :], v_hi[0:rows, half, j, :].bitcast(F32),
                                  ALU.subtract).then_inc(vlo_ready, 1)

            def maximum(s, h, i):
                dve.wait_ge(scored, 2 * s + i + 1)
                _wait(dve, exp_ready, 2 * (s - 1))
                dve.tensor_reduce(nmax[:, h % 2, i:i + 1], ps_s[i][:, 0:KEYS], AX.X, ALU.max,
                                  negate=True).then_inc(max_ready, 1)

            def step(b, h):
                s = HEADS * b + h
                if _live(s, STEPS):
                    maximum(s, h, 0)
                if _live(s - 3, STEPS):
                    hh = (h - 3) % HEADS
                    dve.wait_ge(ohi_ready, s - 2)
                    dve.scalar_tensor_tensor(out=o_lo[:, (h - 3) % 2, :], in0=ps_qa[:, TOK:2 * TOK],
                                             scalar=bkv[:, HEADS + hh:HEADS + hh + 1],
                                             in1=o_hi[:, (h - 3) % 2, :].bitcast(F32), op0=ALU.add,
                                             op1=ALU.subtract).then_inc(olo_ready, 1)
                if _live(s, STEPS):
                    maximum(s, h, 1)
                if _live(s + 1, STEPS):
                    k_part(s + 1, (h + 1) % 2, (h + 1) % HEADS)
                if _live(s, STEPS):
                    if h == 1 and _live(b + 1, BATCH):
                        dve.wait_ge(bn_ready, 3 * b + 7)
                        dve.wait_ge(rstd_ready, b + 1)
                    dve.wait_ge(exp_ready, 2 * s + 2)
                    _wait(dve, norm0_ready, s - 1)
                    dve.reciprocal(rinv[:, h % 2, :], rsum[:, h % 2, :]).then_inc(rinv_ready, 1)
                    if h == 1 and _live(b + 1, BATCH):
                        aggregate(b + 1)
                if _live(s + 1, STEPS):
                    q_part(s + 1, (h + 1) % 2, (h + 1) % HEADS)
                if _live(s, STEPS):
                    dve.wait_ge(rinv_ready, s + 1)
                    dve.tensor_scalar(prob[:, h % 2, 1, 0:KEYS], prob[:, h % 2, 1, 0:KEYS], rinv[:, h % 2, 1:2], None,
                                      ALU.mult).then_inc(norm1_ready, 1)
                if h == 6 and _live(b + 1, BATCH):
                    tokens_lo(b + 1)
                if _live(s - 1, STEPS):
                    dve.wait_ge(pthi_ready, s)
                    dve.tensor_tensor(pt_lo[:, (h - 1) % 2, :], ps_t[:, 0:3 * TOK], pt_hi[:, (h - 1) % 2, :].bitcast(F32),
                                      ALU.subtract).then_inc(ptlo_ready, 1)
                bv = b + 1 if h == 7 else b
                if h in VG_AT and _live(bv, BATCH):
                    v_piece(bv, VG_AT[h])
                if h == 0 and _live(b + 1, BATCH):
                    statistics(b + 1)
                if h == 4 and _live(b + 1, BATCH):
                    normalise(b + 1)
                if h == 2 and _live(b - 1, BATCH):
                    rows = x_all[:, bass.ds(TT * (b - 1), TT), :]
                    dve.wait_ge(projected, HEADS * b)
                    dve.wait_ge(xb_ready, b)
                    dve.scalar_tensor_tensor(out=rows, in0=ps_y[:, :].rearrange("p (i d) -> p i d", i=TT),
                                             scalar=tg[:, 0:1], in1=rows, op0=ALU.mult,
                                             op1=ALU.add).then_inc(x2_ready, 1)

            dve.wait_ge(bn_ready, 1)
            statistics(0)
            dve.wait_ge(bn_ready, 4)
            aggregate(0)
            normalise(0)
            for n in range(4):
                if n == 1:
                    tokens_lo(0)
                dve.wait_ge(whi_ready, n + 1)
                dve.scalar_tensor_tensor(out=piece(w_lo, n), in0=piece(raw, n), scalar=SCALE if n == 0 else 1.0,
                                         in1=piece(w_hi, n).bitcast(F32), op0=ALU.mult,
                                         op1=ALU.subtract).then_inc(wlo_ready, 1)
                if n == 1:
                    k_part(0, 0, 0)
                    q_part(0, 0, 0)
            v_piece(0, 0)
            dve.wait_ge(tg_ready, 1)
            dve.tensor_scalar(tgbo[:, :], bo[:, :], tg[:, 0:1], None, ALU.mult).then_inc(tg_ready, 1)
            for h in range(HEADS):
                step(0, h)
            with dve.Fori(1, BATCH - 1) as b:
                for h in range(HEADS):
                    step(b, h)
            for h in range(HEADS):
                step(BATCH - 1, h)
            for h in range(3):
                step(BATCH, h)

        @block.tensor
        def _(pe):
            def product(out, pairs, first=True, last=True):
                n = 0
                for s_hi, s_lo, m_hi, m_lo in pairs:
                    for a, m in ((s_hi, m_hi), (s_hi, m_lo), (s_lo, m_hi)):
                        n += 1
                        mm = pe.matmul(out, a, m, start=first and n == 1, stop=last and n == 3 * len(pairs))
                return mm

            def turn_tokens(b, c):
                pe.wait_ge(z_ready, 3 * (b + 1))
                if c == 0:
                    _wait(pe, vlo_ready, VGROUPS * b)
                else:
                    pe.wait_ge(tok_scaled, 2 * FC * b + 2)
                for i in range(TT):
                    pe.transpose(ps_v[:, i * P:(i + 1) * P], z[:, i, c * P:(c + 1) * P], ident[:, :])
                pe.transpose(ps_v[:, TOK:KEYS], z[0:MEDIA, 2, c * P:(c + 1) * P], ident[0:MEDIA, 0:MEDIA])\
                  .then_inc(tok_turned, 1)

            def project_qk(u, h, b):
                pe.wait_ge(lnlo_ready, b + 1)
                _wait(pe, qklo_ready, 2 * u - 1)
                product(ps_k[:, 0:KPAD], [(wk(w_hi, c, h), wk(w_lo, c, h), ln_hi[:, c, :], ln_lo[:, c, :])
                                          for c in range(FC)]).then_inc(qk_projected, 1)
                _wait(pe, qklo_ready, 2 * u)
                _wait(pe, olo_ready, u - 3)
                product(ps_qa[:, 0:TOK], [(wq(w_hi, c, h), wq(w_lo, c, h), ln_hi[:, c, 0:TOK], ln_lo[:, c, 0:TOK])
                                          for c in range(FC)]).then_inc(qk_projected, 1)

            def project_v(b, g):
                half, j = divmod(g, 3)
                if g == 0:
                    pe.wait_ge(tok_scaled, 2 * FC * (b + 1))
                else:
                    pe.wait_ge(vlo_ready, VGROUPS * b + g)
                j0, j1 = (j * P, (j + 1) * P) if j < 2 else (TOK, KEYS)
                product(ps_v[0:j1 - j0, :], [(ln_hi[:, c, j0:j1], ln_lo[:, c, j0:j1], wv(w_hi, c, half), wv(w_lo, c, half))
                                             for c in range(FC)]).then_inc(v_projected, 1)

            def step(b, h):
                s = HEADS * b + h
                if _live(s, STEPS):
                    pe.wait_ge(qklo_ready, 2 * (s + 1))
                    for i in range(TT):
                        _wait(pe, exp_ready, 2 * s - 1 + i)
                        product(ps_s[i][:, 0:KPAD], [(q_hi[:, h % 2, i * P:(i + 1) * P], q_lo[:, h % 2, i * P:(i + 1) * P],
                                                      k_hi[:, h % 2, :], k_lo[:, h % 2, :])]).then_inc(scored, 1)
                if _live(s + 1, STEPS):
                    project_qk(s + 1, (h + 1) % HEADS, b + 1 if h == HEADS - 1 else b)
                if _live(s - 1, STEPS):
                    if isinstance(s, int) and s == 1:
                        pe.wait_ge(const_ready, 2)
                    pe.wait_ge(norm0_ready, s)
                    pe.wait_ge(norm1_ready, s)
                    _wait(pe, ptlo_ready, s - 1)
                    for j in range(3):
                        j0, j1 = (j * P, (j + 1) * P) if j < 2 else (TOK, KEYS)
                        for i in range(TT):
                            mm = pe.transpose(ps_t[0:j1 - j0, j * TOK + i * P:j * TOK + (i + 1) * P],
                                              prob[:, (h - 1) % 2, i, j0:j1], ident[:, :])
                    mm.then_inc(p_turned, 1)
                bv = b + 1 if h == 7 else b
                if h in VG_AT and _live(bv, BATCH):
                    project_v(bv, VG_AT[h])
                if h == 5 and _live(b + 1, BATCH):
                    turn_tokens(b + 1, 0)
                if _live(s - 3, STEPS):
                    hh = (h - 3) % HEADS
                    par = (h - 3) % 2
                    if isinstance(s, int) and s == 3:
                        pe.wait_ge(wlo_ready, 4)
                    pe.wait_ge(olo_ready, s - 2)
                    if hh == 0:
                        _wait(pe, x2_ready, b)
                    for i in range(TT):
                        for n, (a, m) in enumerate(((o_hi, w_hi), (o_hi, w_lo), (o_lo, w_hi))):
                            mm = pe.matmul(ps_y[:, i * DIM:(i + 1) * DIM], a[:, par, i * P:(i + 1) * P], wo(m, hh),
                                           start=hh == 0 and i == 0 and n == 0, stop=hh == HEADS - 1 and n == 2,
                                           skip_group_check=True)
                    mm.then_inc(projected, 1)
                if _live(s - 2, STEPS):
                    hh = (h - 2) % HEADS
                    bw = b if h >= 2 else b - 1
                    half, col = hh // 4, (hh % 4) * DH
                    pe.wait_ge(ptlo_ready, s - 1)
                    pe.wait_ge(vlo_ready, VGROUPS * bw + 3 * (half + 1))
                    if _live(s + 1, STEPS):
                        pe.wait_ge(qklo_ready, 2 * (s + 2))
                    _wait(pe, olo_ready, s - 2)
                    product(ps_qa[:, TOK:2 * TOK], [
                        (v_hi[0:r, half, j, col:col + DH], v_lo[0:r, half, j, col:col + DH],
                         pt_hi[0:r, h % 2, j * TOK:(j + 1) * TOK], pt_lo[0:r, h % 2, j * TOK:(j + 1) * TOK])
                        for j, r in enumerate((P, P, MEDIA))]).then_inc(attended, 1)
                if h == 5 and _live(b + 1, BATCH):
                    turn_tokens(b + 1, 1)

            pe.wait_ge(id_ready, 2)
            pe.wait_ge(rows_in, 16 * 6)
            pe.transpose(ps_y[:, 0:VR], vec_rows[:, :], ident[0:VR, 0:VR]).then_inc(rows_turned, 1)
            for c in range(FC):
                turn_tokens(0, c)
            pe.wait_ge(wlo_ready, 2)
            project_qk(0, 0, 0)
            pe.wait_ge(wlo_ready, 3)
            project_v(0, 0)
            for h in range(HEADS):
                step(0, h)
            with pe.Fori(1, BATCH - 1) as b:
                for h in range(HEADS):
                    step(b, h)
            for h in range(HEADS):
                step(BATCH - 1, h)
            for h in range(3):
                step(BATCH, h)


def ffn(nc, t, x_all, ident, raw_gu, raw_down, raw_in):
    with ExitStack() as ctx:
        def sb(name, shape, dt=F32):
            return ctx.enter_context(nc.sbuf_tensor(name, shape, dt))

        def ps(name, shape):
            return ctx.enter_context(nc.psum_tensor(name, shape, F32))

        def sem(name):
            return ctx.enter_context(nc.semaphore(name))

        gu_hi = sb("gu_hi", [P, FC, GU], F32R)
        gu_lo = sb("gu_lo", [P, FC, GU], F32R)
        dn_hi = sb("dn_hi", [P, EXP + 1, DIM], F32R)
        dn_lo = sb("dn_lo", [P, EXP + 1, DIM], F32R)
        gf = sb("gf", [P, 1])
        tgf = sb("tgf", [P, 1])
        bias = sb("bias", [P, EXP])
        bias_half = sb("bias_half", [P, EXP])
        before = sb("before", [P, EXP, EXP])
        mhalf2 = sb("mhalf2", [P, TT])
        eps2 = sb("eps2", [P, TT])
        stats2 = sb("stats2", [P, TT, 6])
        mv2 = sb("mv2", [P, TT, 2])
        rstd = sb("rstd", [P, 2, TT])
        z2 = sb("z2", [P, TT, DIM])
        xt_hi = sb("xt_hi", [P, 2, FC, TOK], F32R)
        xt_lo = sb("xt_lo", [P, 2, FC, TOK], F32R)
        th = sb("th", [P, 2, 512])
        act_a = sb("act_a", [P, 2, 512])
        act_h = sb("act_h", [P, TT, (EXP + 1) * I])
        act_f = sb("act_f", [P, TT, (EXP + 1) * I])
        ft_hi = sb("ft_hi", [P, 2, 512], F32R)
        ft_lo = sb("ft_lo", [P, 2, 512], F32R)
        tl = sb("tl", [P, TT, EXP])
        comb = sb("comb", [P, TT, EXP + 1])
        sig = sb("sig", [P, TT, EXP + 1])
        choice = sb("choice", [P, 2 * TT, 4])
        sums6 = sb("sums6", [P, 2 * TT, 6])
        gsum = sb("gsum", [P, 2 * TT])
        pick = sb("pick", [P, 2 * TT])
        cmp_both = sb("cmp_both", [P, TT * EXP, 2 * EXP])
        rank = sb("rank", [P, TT * EXP])
        wsum = sb("wsum", [P, 2, TT])
        y_out = sb("y_out", [P, 2, DIM])

        ps_g = [ps("ps_g0", [P, 512]), ps("ps_g1", [P, 512])]
        ps_u = [ps("ps_u0", [P, 512]), ps("ps_u1", [P, 512])]
        ps_sh = ps("ps_sh", [P, 512])
        ps_x = ps("ps_x", [P, 512])
        ps_f = ps("ps_f", [P, 512])
        ps_o = ps("ps_o", [P, 512])

        vec_in, ffn_gate, wsplit_hi, wsplit_lo = sem("f_vec_in"), sem("f_gate"), sem("f_wsplit_hi"), sem("f_wsplit_lo")
        masks, half2, consts = sem("f_masks"), sem("f_half"), sem("f_consts")
        bn2, var_ready, rstep, rstd_ready, z_ready = sem("f_bn"), sem("f_var"), sem("f_rstep"), sem("f_rstd"), sem("f_z")
        x_turned, xthi_ready, xtlo_ready = sem("f_x_turned"), sem("f_xthi"), sem("f_xtlo")
        gu_done = sem("f_gu_done")
        tanh_done, a_done, h_done = sem("f_tanh"), sem("f_a"), sem("f_h")
        logit_tanh, comb_ready, route = sem("f_logit_tanh"), sem("f_comb"), sem("f_route")
        f_ready, f_turned, fthi_ready, ftlo_ready = sem("f_f"), sem("f_turned"), sem("f_fthi"), sem("f_ftlo")
        down_done, y_ready, y_stored = sem("f_down"), sem("f_y"), [sem("f_y_stored0"), sem("f_y_stored1")]

        SLOTS = ((0, 2), (0, 0), (1, 2), (0, 1), (1, 0), (1, 1))
        BANK = {(0, 0): 0, (0, 1): 1, (1, 0): 0, (1, 1): 1}
        DOWN = ((0, 0), (0, 1), (0, 2), (1, 0), (1, 1), (1, 2))
        NU = len(SLOTS)
        GC = (0, 1024, 2048)
        ROUTE_STEPS = 16
        DOWN_LAG, DOWN_AT, OUT_LAG = NU + 2, NU + 3, NU + 4

        block = ctx.enter_context(nc.Block())

        @block.sync
        def _(sp):
            sp.dma_start(gf[:, :], t["g_ffn"].unsqueeze(0).to_broadcast([P, 1])).then_inc(vec_in, 16)
            sp.dma_start(bias[:, :], t["L0_ffn_correction_bias"].unsqueeze(0).to_broadcast([P, EXP])).then_inc(vec_in, 16)
            out = t["out"].rearrange("b (i p) d -> b i p d", p=P)

            def store(p):
                for i in range(TT):
                    sp.wait_ge(y_ready, TT * p + i + 1)
                    sp.dma_start(out[bass.ds(p, 1), i].rearrange("o p d -> (o p) d"), y_out[:, i, :]).then_inc(y_stored[i], 16)

            with sp.Fori(0, PAIRS) as p:
                store(p)
            for i in range(TT):
                sp.wait_ge(y_stored[i], 16 * PAIRS)

        @block.gpsimd
        def _(pool):
            pool.memset(mhalf2[:, :], -0.5).then_inc(half2, 1)
            pool.memset(eps2[:, :], EPS).then_inc(half2, 1)
            pool.memset(before[:, :, :], 1.0).then_inc(masks, 1)
            pool.memset(comb[:, :, EXP:EXP + 1], 0.5).then_inc(masks, 1)
            pool.wait_ge(masks, 2)
            pool.affine_select(out=before[:, :, :], in_=before[:, :, :], compare_op=ALU.is_gt, fill=0.0, base=0,
                               pattern=[[1, EXP], [-1, EXP]], channel_multiplier=0).then_inc(masks, 1)

            def reciprocal_deviation(p):
                pool.wait_ge(var_ready, TT * (p + 1))
                _wait(pool, z_ready, TT * p)
                pool.wait_ge(half2, 2)
                pool.tensor_tensor(rstd[:, 0, :], mv2[:, :, 1], eps2[:, :], ALU.add).then_inc(rstep, 1)
                pool.wait_ge(rstep, p + 1)
                pool.tensor_tensor(rstd[:, 1, :], rstd[:, 0, :], mhalf2[:, :], ALU.pow).then_inc(rstd_ready, 1)

            def pair(p, par):
                if _live(p + 1, PAIRS):
                    reciprocal_deviation(p + 1)
                for n, (i, u) in enumerate(SLOTS):
                    pool.wait_ge(h_done, NU * p + n + 1)
                    if n == 0:
                        pool.wait_ge(comb_ready, p + 1)
                        pool.wait_ge(masks, 3)
                    _wait(pool, f_turned, NU * (p - 1) + DOWN.index((i, u)) + 1)
                    e0, ne = UE[u], UN[u]
                    pool.tensor_tensor(act_f[:, i, e0 * I:(e0 + ne) * I].rearrange("p (e i) -> p e i", e=ne),
                                       act_h[:, i, e0 * I:(e0 + ne) * I].rearrange("p (e i) -> p e i", e=ne),
                                       comb[:, i, e0:e0 + ne].unsqueeze(2).to_broadcast([P, ne, I]),
                                       ALU.mult).then_inc(f_ready, 1)

            reciprocal_deviation(0)
            pair(0, 0)
            pair(1, 1)
            with pool.Fori(2, PAIRS - 2, 2) as p:
                pair(p, 0)
                pair(p + 1, 1)
            pair(PAIRS - 2, 0)
            pair(PAIRS - 1, 1)

        def lagged(p, n, lag):
            return p + (n - lag) // NU, (n - lag) % NU

        def place(p, n):
            return NU * p + n

        @block.scalar
        def _(act):
            act.wait_ge(vec_in, 32)
            act.activation(tgf[:, :], gf[:, :], ACT.Tanh).then_inc(ffn_gate, 1)

            def tokens_hi(p, par):
                act.wait_ge(x_turned, p + 1)
                _wait(act, gu_done, NU * (p - 1))
                act.activation(xt_hi[:, par, :, :].rearrange("p c n -> p (c n)"), ps_x[:, :], ACT.Copy).then_inc(xthi_ready, 1)

            def down_hi(p, n):
                d = place(p, n)
                w = UN[DOWN[n][1]] * I
                act.wait_ge(f_turned, d + 1)
                _wait(act, down_done, d - 1)
                act.activation(ft_hi[:, n % 2, 0:w], ps_f[:, 0:w], ACT.Copy).then_inc(fthi_ready, 1)

            def pair(p, par):
                for n, (i, u) in enumerate(SLOTS):
                    w = UN[u] * I
                    act.wait_ge(gu_done, NU * p + n + 1)
                    _wait(act, a_done, NU * p + n - 1)
                    src = ps_sh if u == 2 else ps_g[BANK[i, u]]
                    act.activation(th[:, n % 2, 0:w], src[:, 0:w], ACT.Tanh, scale=0.5).then_inc(tanh_done, 1)
                    if u == 2:
                        _wait(act, comb_ready, p)
                        act.activation(tl[:, i, :], ps_sh[:, 2 * I:2 * I + EXP], ACT.Tanh, scale=0.5).then_inc(logit_tanh, 1)
                    q, m = lagged(p, n, DOWN_LAG)
                    if _live(q, PAIRS):
                        down_hi(q, m)
                    if n == 4 and _live(p + 1, PAIRS):
                        tokens_hi(p + 1, 1 - par)

            act.wait_ge(raw_in, 16 * RAW_DMAS)
            for c0, c1 in ((2048, GU), (0, 1024), (1024, 2048)):
                act.activation(gu_hi[:, :, c0:c1], raw_gu[:, :, c0:c1], ACT.Copy).then_inc(wsplit_hi, 1)
                if c0 == 0:
                    tokens_hi(0, 0)
            act.activation(dn_hi[:, :, :], raw_down[:, :, :], ACT.Copy).then_inc(wsplit_hi, 1)
            pair(0, 0)
            pair(1, 1)
            with act.Fori(2, PAIRS - 2, 2) as p:
                pair(p, 0)
                pair(p + 1, 1)
            pair(PAIRS - 2, 0)
            pair(PAIRS - 1, 1)
            for n in range(DOWN_LAG):
                q, m = lagged(PAIRS, n, DOWN_LAG)
                down_hi(q, m)

        @block.vector
        def _(dve):
            def statistics(p):
                for i in range(TT):
                    dve.bn_stats(stats2[:, i, :], x_all[:, bass.ds(TT * p + i, 1), :].rearrange("p o d -> p (o d)"))\
                       .then_inc(bn2, 1)

            def aggregate(p):
                for i in range(TT):
                    dve.bn_aggr(mv2[:, i, :], stats2[:, i, :]).then_inc(var_ready, 1)

            def normalise(p):
                dve.wait_ge(rstd_ready, p + 1)
                _wait(dve, x_turned, p)
                for i in range(TT):
                    dve.tensor_scalar(z2[:, i, :], x_all[:, bass.ds(TT * p + i, 1), :].rearrange("p o d -> p (o d)"),
                                      mv2[:, i, 0:1], rstd[:, 1, i:i + 1], ALU.subtract, ALU.mult).then_inc(z_ready, 1)

            def tokens_lo(p, par):
                dve.wait_ge(xthi_ready, p + 1)
                dve.tensor_tensor(xt_lo[:, par, :, :].rearrange("p c n -> p (c n)"), ps_x[:, :],
                                  xt_hi[:, par, :, :].rearrange("p c n -> p (c n)").bitcast(F32),
                                  ALU.subtract).then_inc(xtlo_ready, 1)

            def down_lo(p, n):
                d = place(p, n)
                w = UN[DOWN[n][1]] * I
                dve.wait_ge(fthi_ready, d + 1)
                dve.tensor_tensor(ft_lo[:, n % 2, 0:w], ps_f[:, 0:w], ft_hi[:, n % 2, 0:w].bitcast(F32),
                                  ALU.subtract).then_inc(ftlo_ready, 1)

            def output(p, i):
                dve.wait_ge(down_done, place(p, 3 * i + 3))
                _wait(dve, y_stored[i], 16 * p)
                if isinstance(p, int) and p == 0:
                    dve.wait_ge(ffn_gate, 1)
                dve.scalar_tensor_tensor(out=y_out[:, i, :], in0=ps_o[:, 0:DIM], scalar=tgf[:, 0:1],
                                         in1=x_all[:, bass.ds(TT * p + i, 1), :].rearrange("p o d -> p (o d)"),
                                         op0=ALU.mult, op1=ALU.add).then_inc(y_ready, 1)

            flat = choice[:, :, :].rearrange("p a b -> p (a b)")
            by_tile = flat.rearrange("p (i e) -> p i e", i=TT)
            scores = sig[:, :, 0:EXP]
            both = cmp_both[:, :, :].rearrange("p (i e) n -> p i e n", i=TT)

            def choices(p):
                dve.wait_ge(logit_tanh, TT * (p + 1))
                _wait(dve, comb_ready, p)
                dve.scalar_tensor_tensor(out=by_tile, in0=tl[:, :, :], scalar=0.5,
                                         in1=bias_half[:, :].unsqueeze(1).to_broadcast([P, TT, EXP]),
                                         op0=ALU.mult, op1=ALU.add).then_inc(route, 1)
                dve.tensor_scalar(scores, tl[:, :, :], 0.5, 0.5, ALU.mult, ALU.add).then_inc(route, 1)

            def pair_sums(p):
                dve.wait_ge(route, ROUTE_STEPS * p + 2)
                dve.tensor_tensor(sums6[:, :, 0:3], choice[:, :, 0:3], choice[:, :, 1:4], ALU.add).then_inc(route, 1)
                dve.tensor_tensor(sums6[:, :, 3:5], choice[:, :, 0:2], choice[:, :, 2:4], ALU.add).then_inc(route, 1)
                dve.tensor_tensor(sums6[:, :, 5:6], choice[:, :, 0:1], choice[:, :, 3:4], ALU.add).then_inc(route, 1)

            def group_sums(p):
                dve.wait_ge(route, ROUTE_STEPS * p + 5)
                dve.tensor_reduce(gsum[:, :], sums6[:, :, :], AX.X, ALU.max).then_inc(route, 1)

            def pick_group(p):
                dve.wait_ge(route, ROUTE_STEPS * p + 6)
                g = gsum[:, :].rearrange("p (i g) -> p i g", g=2)
                picks = pick[:, :].rearrange("p (i g) -> p i g", g=2)
                dve.tensor_tensor(picks[:, :, 0], g[:, :, 0], g[:, :, 1], ALU.is_ge).then_inc(route, 1)
                dve.tensor_tensor(picks[:, :, 1], g[:, :, 1], g[:, :, 0], ALU.is_gt).then_inc(route, 1)

            def mask_choices(p):
                dve.wait_ge(route, ROUTE_STEPS * p + 8)
                dve.tensor_tensor(choice[:, :, :], choice[:, :, :], pick[:, :].unsqueeze(2).to_broadcast([P, 2 * TT, 4]),
                                  ALU.mult).then_inc(route, 1)

            def compare(p):
                dve.wait_ge(route, ROUTE_STEPS * p + 9)
                other = by_tile.unsqueeze(2).to_broadcast([P, TT, EXP, EXP])
                own = by_tile.unsqueeze(3).to_broadcast([P, TT, EXP, EXP])
                dve.tensor_tensor(both[:, :, :, 0:EXP], other, own, ALU.is_gt).then_inc(route, 1)
                dve.tensor_tensor(both[:, :, :, EXP:], other, own, ALU.is_equal).then_inc(route, 1)

            def break_ties(p):
                dve.wait_ge(route, ROUTE_STEPS * p + 11)
                dve.tensor_tensor(both[:, :, :, EXP:], both[:, :, :, EXP:],
                                  before[:, :, :].unsqueeze(1).to_broadcast([P, TT, EXP, EXP]), ALU.mult).then_inc(route, 1)

            def ranks(p):
                dve.wait_ge(route, ROUTE_STEPS * p + 12)
                dve.tensor_reduce(rank[:, :], cmp_both[:, :, :], AX.X, ALU.add).then_inc(route, 1)

            def select_scores(p):
                dve.wait_ge(route, ROUTE_STEPS * p + 13)
                dve.scalar_tensor_tensor(out=scores, in0=rank[:, :].rearrange("p (i e) -> p i e", i=TT), scalar=2.0,
                                         in1=scores, op0=ALU.is_lt, op1=ALU.mult).then_inc(route, 1)

            def score_sum(p):
                dve.wait_ge(route, ROUTE_STEPS * p + 14)
                dve.tensor_reduce(wsum[:, 0, :], sig[:, :, :], AX.X, ALU.add).then_inc(route, 1)

            def invert_sum(p):
                dve.wait_ge(route, ROUTE_STEPS * p + 15)
                dve.reciprocal(wsum[:, 1, :], wsum[:, 0, :]).then_inc(route, 1)

            def weights(p):
                dve.wait_ge(route, ROUTE_STEPS * p + 16)
                _wait(dve, f_ready, NU * p)
                dve.scalar_tensor_tensor(out=comb[:, :, 0:EXP], in0=scores, scalar=0.5,
                                         in1=wsum[:, 1, :].unsqueeze(2).to_broadcast([P, TT, EXP]),
                                         op0=ALU.mult, op1=ALU.mult).then_inc(comb_ready, 1)

            ROUTING = {2: ((), (choices,), (pair_sums,)),
                       3: ((group_sums,), (pick_group,), (mask_choices,)),
                       4: ((compare,), (break_ties, ranks), (select_scores, score_sum, invert_sum, weights))}

            def pair(p, par):
                for n, (i, u) in enumerate(SLOTS):
                    w, e0 = UN[u] * I, UE[u]
                    q, m = lagged(p, n, OUT_LAG)
                    if m % 3 == 2 and _live(q, PAIRS):
                        output(q, m // 3)
                    if n == 3 and _live(p + 1, PAIRS):
                        normalise(p + 1)
                    if n == 5 and _live(p + 1, PAIRS):
                        tokens_lo(p + 1, 1 - par)
                    if n == 1 and _live(p + 1, PAIRS):
                        dve.wait_ge(bn2, TT * (p + 2))
                        dve.wait_ge(rstd_ready, p + 1)
                    g_bank = ps_sh[:, 0:w] if u == 2 else ps_g[BANK[i, u]][:, 0:w]
                    u_bank = ps_sh[:, w:2 * w] if u == 2 else ps_u[BANK[i, u]][:, 0:w]
                    dve.wait_ge(tanh_done, NU * p + n + 1)
                    if u == 2:
                        dve.wait_ge(logit_tanh, TT * p + (n > 0) + 1)
                    _wait(dve, h_done, NU * p + n - 1)
                    dve.scalar_tensor_tensor(out=act_a[:, n % 2, 0:w], in0=th[:, n % 2, 0:w], scalar=1.0, in1=g_bank,
                                             op0=ALU.add, op1=ALU.mult).then_inc(a_done, 1)
                    if n == 1 and _live(p + 1, PAIRS):
                        aggregate(p + 1)
                    for routing in ROUTING.get(n, ((),) * 3)[0]:
                        routing(p)
                    dve.wait_ge(a_done, NU * p + n + 1)
                    _wait(dve, f_ready, NU * (p - 1) + n + 1)
                    dve.tensor_tensor(act_h[:, i, e0 * I:e0 * I + w], act_a[:, n % 2, 0:w], u_bank,
                                      ALU.mult).then_inc(h_done, 1)
                    for routing in ROUTING.get(n, ((),) * 3)[1]:
                        routing(p)
                    q, m = lagged(p, n, DOWN_LAG)
                    if _live(q, PAIRS):
                        down_lo(q, m)
                    for routing in ROUTING.get(n, ((),) * 3)[2]:
                        routing(p)
                    if n == 0 and _live(p + 1, PAIRS):
                        statistics(p + 1)

            statistics(0)
            dve.wait_ge(bn2, TT)
            aggregate(0)
            dve.wait_ge(vec_in, 32)
            dve.tensor_scalar(bias_half[:, :], bias[:, :], 0.5, None, ALU.add).then_inc(consts, 1)
            dve.memset(sig[:, :, EXP:EXP + 1], 1e-20).then_inc(consts, 1)
            for n, (c0, c1) in enumerate(((2048, GU), (0, 1024), (1024, 2048))):
                dve.wait_ge(wsplit_hi, n + 1)
                dve.tensor_tensor(gu_lo[:, :, c0:c1], raw_gu[:, :, c0:c1], gu_hi[:, :, c0:c1].bitcast(F32),
                                  ALU.subtract).then_inc(wsplit_lo, 1)
                if n == 0:
                    normalise(0)
                if n == 1:
                    tokens_lo(0, 0)
            dve.wait_ge(wsplit_hi, 4)
            dve.tensor_tensor(dn_lo[:, :, :], raw_down[:, :, :], dn_hi[:, :, :].bitcast(F32),
                              ALU.subtract).then_inc(wsplit_lo, 1)
            dve.wait_ge(consts, 2)
            dve.wait_ge(masks, 3)
            pair(0, 0)
            pair(1, 1)
            with dve.Fori(2, PAIRS - 2, 2) as p:
                pair(p, 0)
                pair(p + 1, 1)
            pair(PAIRS - 2, 0)
            pair(PAIRS - 1, 1)
            for n in range(OUT_LAG):
                q, m = lagged(PAIRS, n, OUT_LAG)
                if m % 3 == 2:
                    output(q, m // 3)
                q, m = lagged(PAIRS, n, DOWN_LAG)
                if q < PAIRS:
                    down_lo(q, m)

        @block.tensor
        def _(pe):
            def turn_tokens(p):
                pe.wait_ge(z_ready, TT * (p + 1))
                _wait(pe, xtlo_ready, p)
                for c in range(FC):
                    for i in range(TT):
                        mm = pe.transpose(ps_x[:, c * TOK + i * P:c * TOK + (i + 1) * P], z2[:, i, c * P:(c + 1) * P], ident[:, :])
                mm.then_inc(x_turned, 1)

            def gate_up(p, par, n):
                i, u = SLOTS[n]
                tok = slice(i * P, (i + 1) * P)
                last = {0: NU * (p - 1) + 3, 1: NU * (p - 1) + 5, 2: NU * p + 1, 3: NU * (p - 1) + 6,
                        4: NU * p + 2, 5: NU * p + 4}[n]
                _wait(pe, h_done, last)
                if n == 0:
                    pe.wait_ge(xtlo_ready, p + 1)
                w = 2 * I + EXP if u == 2 else 512
                banks = [(ps_sh, GC[2])] if u == 2 else [(ps_g[BANK[i, u]], GC[u]), (ps_u[BANK[i, u]], GC[u] + 512)]
                for bank, c0 in banks:
                    k = 0
                    for c in range(FC):
                        for a, m in ((xt_hi, gu_hi), (xt_hi, gu_lo), (xt_lo, gu_hi)):
                            mm = pe.matmul(bank[:, 0:w], a[:, par, c, tok], m[:, c, c0:c0 + w], start=k == 0, stop=k == 5)
                            k += 1
                mm.then_inc(gu_done, 1)

            def turn_f(p, n):
                i, u = DOWN[n]
                d = place(p, n)
                pe.wait_ge(f_ready, NU * p + SLOTS.index((i, u)) + 1)
                _wait(pe, ftlo_ready, d)
                for k in range(UN[u]):
                    e = UE[u] + k
                    mm = pe.transpose(ps_f[:, k * P:(k + 1) * P], act_f[:, i, e * I:(e + 1) * I], ident[:, :])
                mm.then_inc(f_turned, 1)

            def down(p, n):
                i, u = DOWN[n]
                pe.wait_ge(ftlo_ready, place(p, n) + 1)
                if u == 0:
                    _wait(pe, y_ready, TT * p + i)
                for k in range(UN[u]):
                    e = UE[u] + k
                    for m, (a, wd) in enumerate(((ft_hi, dn_hi), (ft_hi, dn_lo), (ft_lo, dn_hi))):
                        mm = pe.matmul(ps_o[:, 0:DIM], a[:, n % 2, k * P:(k + 1) * P], wd[:, e, :],
                                       start=u == 0 and k == 0 and m == 0, stop=u == 2 and m == 2)
                mm.then_inc(down_done, 1)

            def pair(p, par):
                for n in range(NU):
                    if isinstance(p, int) and p == 0 and n in (0, 1, 3):
                        pe.wait_ge(wsplit_lo, {0: 1, 1: 2, 3: 3}[n])
                    gate_up(p, par, n)
                    q, m = lagged(p, n, DOWN_AT)
                    if _live(q, PAIRS):
                        if isinstance(q, int) and q == 0 and m == 0:
                            pe.wait_ge(wsplit_lo, 4)
                        down(q, m)
                    if n == 4 and _live(p + 1, PAIRS):
                        turn_tokens(p + 1)
                    q, m = lagged(p, n, DOWN_LAG)
                    if _live(q, PAIRS):
                        turn_f(q, m)

            turn_tokens(0)
            pair(0, 0)
            pair(1, 1)
            with pe.Fori(2, PAIRS - 2, 2) as p:
                pair(p, 0)
                pair(p + 1, 1)
            pair(PAIRS - 2, 0)
            pair(PAIRS - 1, 1)
            for n in range(DOWN_AT):
                q, m = lagged(PAIRS, n, DOWN_AT)
                down(q, m)
                q, m = lagged(PAIRS, n, DOWN_LAG)
                if q < PAIRS:
                    turn_f(q, m)


def load_ffn_weights(engine, t, raw_gu, raw_down, raw_in):
    for c in range(FC):
        rows = slice(c * P, (c + 1) * P)
        for half in range(2):
            for k, name in enumerate(("w_gate", "w_up")):
                engine.dma_start(raw_gu[:, c, half * 1024 + k * 512:half * 1024 + (k + 1) * 512].rearrange("p (e i) -> p e i", e=4),
                                 t["L0_ffn_" + name][half * 4:half * 4 + 4, rows, :].rearrange("e p i -> p e i")).then_inc(raw_in, 16)
    for k, name in enumerate(("sw_gate", "sw_up")):
        engine.dma_start(raw_gu[:, :, 2048 + k * I:2048 + (k + 1) * I],
                         t["L0_ffn_" + name].rearrange("(c p) i -> p c i", p=P)).then_inc(raw_in, 16)
    engine.dma_start(raw_down[:, 0:EXP, :], t["L0_ffn_w_down"].rearrange("e p d -> p e d")).then_inc(raw_in, 16)
    engine.dma_start(raw_down[:, EXP, :], t["L0_ffn_sw_down"]).then_inc(raw_in, 16)
    for c in range(FC):
        engine.dma_start(raw_gu[:, c, 2048 + 2 * I:GU],
                         t["L0_ffn_router_weight"][:, c * P:(c + 1) * P].rearrange("e p -> p e"),
                         allow_slow_non_contiguous=True).then_inc(raw_in, 16)


def build(nc, t):
    with ExitStack() as ctx:
        x_all = ctx.enter_context(nc.sbuf_tensor("x_all", [P, TT * BATCH, DIM], F32))
        ident = ctx.enter_context(nc.sbuf_tensor("ident", [P, P], F32))
        raw = ctx.enter_context(nc.sbuf_tensor("raw", [P, RAW], F32))
        raw_in = ctx.enter_context(nc.semaphore("raw_in"))
        raw_gu = raw[:, 0:FC * GU].rearrange("p (c n) -> p c n", c=FC)
        raw_down = raw[:, FC * GU:FC * GU + (EXP + 1) * DIM].rearrange("p (e d) -> p e d", e=EXP + 1)
        attention(nc, t, x_all, ident, raw, lambda engine: load_ffn_weights(engine, t, raw_gu, raw_down, raw_in))
        ffn(nc, t, x_all, ident, raw_gu, raw_down, raw_in)


_INS = ['x', 'ctx_1024', 'g_xattn', 'g_ffn', 'L0_xattn_gamma_media', 'L0_xattn_beta_media', 'L0_xattn_gamma_lat',
        'L0_xattn_beta_lat', 'L0_xattn_Wq', 'L0_xattn_bq', 'L0_xattn_Wkv', 'L0_xattn_bkv', 'L0_xattn_Wo', 'L0_xattn_bo',
        'L0_ffn_router_weight', 'L0_ffn_correction_bias', 'L0_ffn_w_gate', 'L0_ffn_w_up', 'L0_ffn_w_down',
        'L0_ffn_sw_gate', 'L0_ffn_sw_up', 'L0_ffn_sw_down']


def kernel(**inputs):
    import numpy as _np
    import concourse.bacc as _bacc
    from concourse import mybir as _mybir
    from concourse.bass_utils import run_bass_kernel_spmd as _run

    nc = _bacc.Bacc("TRN2", target_bir_lowering=False, num_devices=1)
    arrays, t = {}, {}
    for name in _INS:
        a = _np.ascontiguousarray(inputs[name])
        arrays[f"in_{name}_dram"] = a
        t[name] = nc.dram_tensor(f"in_{name}_dram", a.shape, _mybir.dt.from_np(a.dtype), kind="ExternalInput").ap()
    t["out"] = nc.dram_tensor("out_0_dram", (BATCH, TOK, DIM), F32, kind="ExternalOutput").ap()
    build(nc, t)
    r = _run(nc, [arrays], core_ids=[0])
    return r.results[0]["out_0_dram"]
```

```python
from contextlib import ExitStack

import concourse.bass as bass
from concourse import mybir

F32 = mybir.dt.float32
F32R = mybir.dt.float32r
ALU = mybir.AluOpType
ACT = mybir.ActivationFunctionType
AX = mybir.AxisListType

P = 128
EPS = 1e-5
BATCH, TOK, DIM = 16, 256, 256
MEDIA = 77
HEADS, DH = 8, 128
INNER = HEADS * DH
KEYS = TOK + MEDIA
KPAD = KEYS + 1
FC = DIM // P
TT = TOK // P
STEPS = BATCH * HEADS
VGROUPS = 6
VG_AT = {7: 0, 0: 1, 1: 2, 2: 3, 3: 4, 4: 5}
SCALE = float(DH) ** -0.5

EXP, I = 8, 128
RAW = 3 * FC * INNER + HEADS * DIM
GU = 2 * (EXP + 1) * I + EXP
RAW_DMAS = 14
PAIRS = BATCH


def _wait(engine, sem, n):
    if not isinstance(n, int) or n > 0:
        engine.wait_ge(sem, n)


def _live(n, end):
    return not isinstance(n, int) or 0 <= n < end


def attention(nc, t, x_all, ident, z, raw, load_ffn):
    with ExitStack() as ctx:
        def sb(name, shape, dt=F32):
            return ctx.enter_context(nc.sbuf_tensor(name, shape, dt))

        def ps(name, shape):
            return ctx.enter_context(nc.psum_tensor(name, shape, F32))

        def sem(name):
            return ctx.enter_context(nc.semaphore(name))

        def tiles(b):
            return TT if isinstance(b, int) and b == BATCH else TT + 1

        QO, KVO, OO = 0, FC * INNER, 3 * FC * INNER
        WN = OO + HEADS * DIM
        w_hi = sb("w_hi", [P, WN], F32R)
        w_lo = sb("w_lo", [P, WN], F32R)
        def wide(w, n):
            if n == 0:
                return w[:, QO:KVO].rearrange("p (c n) -> p c n", c=FC)
            if n == 3:
                return w[:, OO:WN].rearrange("p (c n) -> p c n", c=HEADS)
            return w[:, KVO:OO].rearrange("p (c n) -> p c n", c=FC)[:, :, (n - 1) * INNER:n * INNER]

        PIECES = ((1, 0), (0, 0), (2, 0), (2, 1), (0, 1), (1, 1), (3, 0), (3, 1))
        HI_AT = {0: (3, 4), 1: (5, 6), 2: (7,)}
        DVE_LO, DVE_LO_AT = (0, 1, 2, 4), {0: (4,)}
        POOL_LO, POOL_LO_AT = (3, 5, 6, 7), {0: (3,), 1: (5,), 2: (6,), 3: (7,)}

        def piece(w, n):
            which, half = PIECES[n]
            if which == 3:
                return wide(w, 3)[:, half * 4:half * 4 + 4, :]
            return wide(w, which)[:, :, half * 512:half * 512 + 512]

        def wq(w, c, h):
            return wide(w, 0)[:, c, h * DH:(h + 1) * DH]

        def wk(w, c, h):
            return wide(w, 1)[:, c, h * DH:(h + 1) * DH]

        def wv(w, c, half):
            return wide(w, 2)[:, c, half * 512:(half + 1) * 512]

        def wo(w, h):
            return wide(w, 3)[:, h, :]

        VR = 4 * FC + 3 * HEADS
        vec_rows = sb("vec_rows", [VR, P])
        vecs = sb("vecs", [P, VR])
        gb = vecs[:, 0:4 * FC].rearrange("p (n c) -> p n c", n=4)
        bkv = vecs[:, 4 * FC + HEADS:VR]
        bqs = sb("bqs", [P, HEADS])
        bo = sb("bo", [P, DIM])
        tgbo = sb("tgbo", [P, DIM])
        gx = sb("gx", [P, 1])
        tg = sb("tg", [P, 1])
        ctx_in = sb("ctx_in", [MEDIA, DIM])
        stats = sb("stats", [P, 3, 6])
        mv = sb("mv", [P, 3, 2])
        rs = sb("rs", [P, 5, 3])
        mhalf = sb("mhalf", [P, 3])
        eps3 = sb("eps3", [P, 3])
        lnf = sb("lnf", [P, FC, KPAD])
        ln_hi = sb("ln_hi", [P, FC, KPAD], F32R)
        ln_lo = sb("ln_lo", [P, FC, KPAD], F32R)
        q_hi = sb("q_hi", [P, 2, TOK], F32R)
        q_lo = sb("q_lo", [P, 2, TOK], F32R)
        k_hi = sb("k_hi", [P, 2, KPAD], F32R)
        k_lo = sb("k_lo", [P, 2, KPAD], F32R)
        v_hi = sb("v_hi", [P, 2, 3, 512], F32R)
        v_lo = sb("v_lo", [P, 2, 3, 512], F32R)
        prob = sb("prob", [P, 2, TT, KPAD])
        nmax = sb("nmax", [P, 2, TT])
        rsum = sb("rsum", [P, 2, TT])
        rinv = sb("rinv", [P, 2, TT])
        pt_hi = sb("pt_hi", [P, 2, 3 * TOK], F32R)
        pt_lo = sb("pt_lo", [P, 2, 3 * TOK], F32R)
        o_hi = sb("o_hi", [P, 2, TOK], F32R)
        o_lo = sb("o_lo", [P, 2, TOK], F32R)

        ps_s = [ps("ps_s0", [P, 512]), ps("ps_s1", [P, 512])]
        ps_qa = ps("ps_qa", [P, 512])
        ps_k = ps("ps_k", [P, 512])
        ps_v = ps("ps_v", [P, 512])
        ps_t = ps("ps_t", [P, 1024])
        ps_y = ps("ps_y", [P, 512])

        def av(s):
            return ps_k if isinstance(s, int) and s == STEPS - 1 else ps_qa

        x_in = [sem("x_in0"), sem("x_in1"), sem("x_in2")]
        vec_in, media_in = sem("vec_in"), sem("media_in")
        rows_in, rows_turned = sem("rows_in"), sem("rows_turned")
        w_in = [sem(f"w_in{n}") for n in range(len(PIECES))]
        id_ready, const_ready, tg_ready = sem("id_ready"), sem("const_ready"), sem("tg_ready")
        bias_ready, half_ready = sem("bias_ready"), sem("half_ready")
        whi_ready, wlo_ready, wlo_pool = sem("whi_ready"), sem("wlo_ready"), sem("wlo_pool")
        stats_ready, rstd_ready, rstd_step, z_ready = sem("stats_ready"), sem("rstd_ready"), sem("rstd_step"), sem("z_ready")
        bn_ready = sem("bn_ready")
        tok_turned, tok_scaled, lnhi_ready, lnlo_ready = sem("tok_turned"), sem("tok_scaled"), sem("lnhi_ready"), sem("lnlo_ready")
        qk_projected, qhi_ready, khi_ready, qklo_ready = sem("qk_projected"), sem("qhi_ready"), sem("khi_ready"), sem("qklo_ready")
        v_projected, vhi_ready, vlo_ready = sem("v_projected"), sem("vhi_ready"), sem("vlo_ready")
        scored, max_ready, exp_ready, rinv_ready = sem("scored"), sem("max_ready"), sem("exp_ready"), sem("rinv_ready")
        norm0_ready, norm1_ready = sem("norm0_ready"), sem("norm1_ready")
        p_turned, pthi_ready, ptlo_ready = sem("p_turned"), sem("pthi_ready"), sem("ptlo_ready")
        attended, ohi_ready, olo_ready = sem("attended"), sem("ohi_ready"), sem("olo_ready")
        projected, xb_ready, x2_ready = sem("projected"), sem("xb_ready"), sem("x2_ready")

        block = ctx.enter_context(nc.Block())

        @block.sync
        def _(sp):
            x_tiles = t["x"].rearrange("b (i p) d -> p (b i) d", p=P)
            sp.dma_start(x_all[:, 0:TT, :], x_tiles[:, 0:TT, :]).then_inc(x_in[0], 16)
            sp.dma_start(ctx_in[:, :], t["ctx_1024"][0]).then_inc(media_in, 16)
            row = 0
            for name, rows in (("gamma_lat", FC), ("beta_lat", FC), ("gamma_media", FC), ("beta_media", FC),
                               ("bq", HEADS), ("bkv", 2 * HEADS)):
                sp.dma_start(vec_rows[row:row + rows, :],
                             t["L0_xattn_" + name].rearrange("(r p) -> r p", p=P)).then_inc(rows_in, 16)
                row += rows
            source = {0: t["L0_xattn_Wq"].rearrange("(c p) n -> p c n", p=P),
                      3: t["L0_xattn_Wo"].rearrange("(c p) n -> p c n", p=P)}
            kv = t["L0_xattn_Wkv"].rearrange("(c p) n -> p c n", p=P)
            source[1], source[2] = kv[:, :, 0:INNER], kv[:, :, INNER:2 * INNER]
            for n, (which, half) in enumerate(PIECES):
                src = source[which]
                src = src[:, half * 4:half * 4 + 4, :] if which == 3 else src[:, :, half * 512:half * 512 + 512]
                sp.dma_start(piece(raw, n), src).then_inc(w_in[n], 16)
                if n == 2:
                    sp.dma_start(x_all[:, TT:2 * TT, :], x_tiles[:, TT:2 * TT, :]).then_inc(x_in[1], 16)
            sp.wait_ge(z_ready, 3)
            sp.dma_start(ctx_in[:, :], t["ctx_1024"][1]).then_inc(media_in, 16)
            sp.dma_start(x_all[:, 2 * TT:, :], x_tiles[:, 2 * TT:, :]).then_inc(x_in[2], 16)
            sp.wait_ge(wlo_ready, len(DVE_LO))
            sp.wait_ge(wlo_pool, len(POOL_LO))
            load_ffn(sp)
            with sp.Fori(2, BATCH) as b:
                sp.wait_ge(z_ready, 3 * b)
                sp.dma_start(ctx_in[:, :], t["ctx_1024"][bass.ds(b, 1)].rearrange("o j d -> (o j) d")).then_inc(media_in, 16)

        @block.gpsimd
        def _(pool):
            pool.memset(ident[:, :], 0.0).then_inc(id_ready, 1)
            pool.memset(mhalf[:, :], -0.5).then_inc(half_ready, 1)
            pool.memset(eps3[:, :], EPS).then_inc(half_ready, 1)
            pool.wait_ge(id_ready, 1)
            pool.affine_select(out=ident[:, :], in_=ident[:, :], compare_op=ALU.not_equal, fill=1.0, base=0,
                               pattern=[[-1, P]], channel_multiplier=1).then_inc(id_ready, 1)

            def reciprocal_deviations(b):
                ve, r1, sq, ve2, rr = (rs[:, n, :] for n in range(5))
                pool.wait_ge(stats_ready, 3 * b + tiles(b))
                _wait(pool, z_ready, 3 * b)
                pool.wait_ge(half_ready, 2)
                var = mv[:, :, 1]
                pool.tensor_tensor(ve, var, eps3[:, :], ALU.add).then_inc(rstd_step, 1)
                pool.wait_ge(rstd_step, 6 * b + 1)
                pool.tensor_tensor(r1, ve, mhalf[:, :], ALU.pow).then_inc(rstd_step, 1)
                pool.wait_ge(rstd_step, 6 * b + 2)
                pool.tensor_tensor(sq, r1, r1, ALU.mult).then_inc(rstd_step, 1)
                pool.wait_ge(rstd_step, 6 * b + 3)
                pool.tensor_tensor(sq, sq, var, ALU.mult).then_inc(rstd_step, 1)
                pool.wait_ge(rstd_step, 6 * b + 4)
                pool.tensor_tensor(ve2, sq, eps3[:, :], ALU.add).then_inc(rstd_step, 1)
                pool.wait_ge(rstd_step, 6 * b + 5)
                pool.tensor_tensor(sq, ve2, mhalf[:, :], ALU.pow).then_inc(rstd_step, 1)
                pool.wait_ge(rstd_step, 6 * b + 6)
                pool.tensor_tensor(rr, r1, sq, ALU.mult).then_inc(rstd_ready, 1)

            def step(b, h):
                s = HEADS * b + h
                pool.wait_ge(rinv_ready, s + 1)
                pool.tensor_tensor(prob[:, h % 2, 0, 0:KEYS], prob[:, h % 2, 0, 0:KEYS],
                                   rinv[:, h % 2, 0:1].to_broadcast([P, KEYS]), ALU.mult).then_inc(norm0_ready, 1)
                if h == 2 and _live(b + 1, BATCH + 1):
                    reciprocal_deviations(b + 1)
                if h == 4:
                    rows = x_all[:, bass.ds(TT * b, TT), :]
                    pool.wait_ge(z_ready, 3 * (b + 1))
                    pool.wait_ge(tg_ready, 2)
                    pool.tensor_tensor(rows, rows, tgbo[:, :].unsqueeze(1).to_broadcast([P, TT, DIM]),
                                       ALU.add).then_inc(xb_ready, 1)

            def split_lo(n):
                pool.wait_ge(whi_ready, n + 1)
                pool.tensor_tensor(piece(w_lo, n), piece(raw, n), piece(w_hi, n).bitcast(F32),
                                   ALU.subtract).then_inc(wlo_pool, 1)

            reciprocal_deviations(0)
            for h in range(HEADS):
                step(0, h)
                for n in POOL_LO_AT.get(h, ()):
                    split_lo(n)
            with pool.Fori(1, BATCH - 1) as b:
                for h in range(HEADS):
                    step(b, h)
            for h in range(HEADS):
                step(BATCH - 1, h)

        @block.scalar
        def _(act):
            act.dma_start(gx[:, :], t["g_xattn"].unsqueeze(0).to_broadcast([P, 1])).then_inc(vec_in, 16)
            act.dma_start(bo[:, :], t["L0_xattn_bo"].unsqueeze(0).to_broadcast([P, DIM])).then_inc(vec_in, 16)
            act.wait_ge(vec_in, 32)
            act.activation(tg[:, :], gx[:, :], ACT.Tanh).then_inc(tg_ready, 1)
            act.wait_ge(rows_turned, 1)
            act.activation(vecs[:, :], ps_y[:, 0:VR], ACT.Copy).then_inc(bias_ready, 1)
            act.wait_ge(bias_ready, 1)
            act.activation(bqs[:, :], vecs[:, 4 * FC:4 * FC + HEADS], ACT.Copy, scale=SCALE).then_inc(bias_ready, 1)

            def turned_tokens(b, c, bank=ps_v):
                act.wait_ge(tok_turned, FC * b + c + 1)
                _wait(act, lnlo_ready, b)
                act.activation(lnf[:, c, 0:TOK], bank[:, 0:TOK], ACT.Identity, bias=gb[:, 1, c:c + 1],
                               scale=gb[:, 0, c:c + 1]).then_inc(tok_scaled, 1)
                act.activation(lnf[:, c, TOK:KEYS], bank[:, TOK:KEYS], ACT.Identity, bias=gb[:, 3, c:c + 1],
                               scale=gb[:, 2, c:c + 1]).then_inc(tok_scaled, 1)

            def tokens_hi(b):
                act.wait_ge(tok_scaled, 2 * FC * (b + 1))
                _wait(act, qk_projected, 2 * HEADS * b)
                _wait(act, v_projected, VGROUPS * b)
                act.activation(ln_hi[:, :, :], lnf[:, :, :], ACT.Copy).then_inc(lnhi_ready, 1)

            def k_part(u, par, h):
                act.wait_ge(qk_projected, 2 * u + 1)
                _wait(act, scored, 2 * (u - 1))
                act.activation(k_hi[:, par, :], ps_k[:, 0:KPAD], ACT.Identity,
                               bias=bkv[:, h:h + 1]).then_inc(khi_ready, 1)

            def q_part(u, par, h):
                act.wait_ge(qk_projected, 2 * u + 2)
                act.activation(q_hi[:, par, :], ps_qa[:, 0:TOK], ACT.Identity,
                               bias=bqs[:, h:h + 1]).then_inc(qhi_ready, 1)

            def v_piece(b, g):
                half, j = divmod(g, 3)
                act.wait_ge(v_projected, VGROUPS * b + g + 1)
                _wait(act, attended, HEADS * b - 4 + 4 * half)
                rows = P if j < 2 else MEDIA
                act.activation(v_hi[0:rows, half, j, :], ps_v[0:rows, :], ACT.Copy).then_inc(vhi_ready, 1)

            def exponentials(s, h, i):
                act.wait_ge(max_ready, 2 * s + i + 1)
                _wait(act, p_turned, s - 1)
                act.activation(prob[:, h % 2, i, 0:KEYS], ps_s[i][:, 0:KEYS], ACT.Exp,
                               bias=nmax[:, h % 2, i:i + 1],
                               accum_out=rsum[:, h % 2, i:i + 1]).then_inc(exp_ready, 1)

            def step(b, h):
                s = HEADS * b + h
                if _live(s - 3, STEPS):
                    hh = (h - 3) % HEADS
                    act.wait_ge(attended, s - 2)
                    _wait(act, projected, s - 4)
                    act.activation(o_hi[:, (h - 3) % 2, :], av(s - 3)[:, TOK:2 * TOK], ACT.Identity,
                                   bias=bkv[:, HEADS + hh:HEADS + hh + 1]).then_inc(ohi_ready, 1)
                if _live(s, STEPS):
                    if h == 6 and _live(b + 1, BATCH):
                        turned_tokens(b + 1, 1)
                    exponentials(s, h, 0)
                if _live(s + 1, STEPS):
                    k_part(s + 1, (h + 1) % 2, (h + 1) % HEADS)
                if _live(s, STEPS):
                    exponentials(s, h, 1)
                if _live(s + 1, STEPS):
                    q_part(s + 1, (h + 1) % 2, (h + 1) % HEADS)
                if h == 6 and _live(b + 1, BATCH):
                    tokens_hi(b + 1)
                if _live(s - 1, STEPS):
                    act.wait_ge(p_turned, s)
                    _wait(act, attended, s - 2)
                    act.activation(pt_hi[:, (h - 1) % 2, :], ps_t[:, 0:3 * TOK], ACT.Copy).then_inc(pthi_ready, 1)
                bv = b + 1 if h == 7 else b
                if h in VG_AT and _live(bv, BATCH):
                    v_piece(bv, VG_AT[h])
                if h == 5 and _live(b + 1, BATCH):
                    turned_tokens(b + 1, 0)

            def split_hi(n):
                act.wait_ge(w_in[n], 16)
                act.activation(piece(w_hi, n), piece(raw, n), ACT.Copy,
                               scale=SCALE if PIECES[n][0] == 0 else 1.0).then_inc(whi_ready, 1)

            act.wait_ge(const_ready, 2)
            split_hi(0)
            for c, bank in enumerate((ps_v, ps_k)):
                turned_tokens(0, c, bank)
            tokens_hi(0)
            split_hi(1)
            split_hi(2)
            act.wait_ge(bias_ready, 2)
            k_part(0, 0, 0)
            q_part(0, 0, 0)
            v_piece(0, 0)
            for h in range(HEADS):
                step(0, h)
                for n in HI_AT.get(h, ()):
                    split_hi(n)
            with act.Fori(1, BATCH - 1) as b:
                for h in range(HEADS):
                    step(b, h)
            for h in range(HEADS):
                step(BATCH - 1, h)
            for h in range(3):
                step(BATCH, h)

        @block.vector
        def _(dve):
            dve.memset(mv[:, :, :], 1.0).then_inc(bn_ready, 1)
            dve.memset(lnf[:, :, KEYS:KPAD], 0.0).then_inc(const_ready, 1)
            dve.memset(ps_t[:, :], 0.0).then_inc(const_ready, 1)

            def latents(b, i):
                return x_all[:, bass.ds(i if tiles(b) == TT else TT * b + i, 1), :].rearrange("p o d -> p (o d)")

            def statistics(b):
                if tiles(b) == TT:
                    dve.wait_ge(x2_ready, 1)
                else:
                    dve.wait_ge(x_in[min(b, 2) if isinstance(b, int) else 2], 16)
                for i in range(TT):
                    dve.bn_stats(stats[:, i, :], latents(b, i)).then_inc(bn_ready, 1)
                if tiles(b) == TT:
                    return
                dve.wait_ge(media_in, 16 * (b + 1))
                dve.bn_stats(stats[0:MEDIA, 2, :], ctx_in[:, :]).then_inc(bn_ready, 1)

            def aggregate(b):
                for i in range(tiles(b)):
                    rows = P if i < 2 else MEDIA
                    dve.bn_aggr(mv[0:rows, i, :], stats[0:rows, i, :]).then_inc(stats_ready, 1)

            def normalise(b):
                dve.wait_ge(rstd_ready, b + 1)
                _wait(dve, tok_turned, FC * b)
                by = 1 if tiles(b) == TT else 4
                for i in range(TT):
                    dve.tensor_scalar(z[:, i, :], latents(b, i), mv[:, i, 0:1], rs[:, by, i:i + 1],
                                      ALU.subtract, ALU.mult).then_inc(z_ready, 1)
                if tiles(b) == TT:
                    return
                dve.tensor_scalar(z[0:MEDIA, 2, :], ctx_in[:, :], mv[0:MEDIA, 2, 0:1], rs[0:MEDIA, 1, 2:3],
                                  ALU.subtract, ALU.mult).then_inc(z_ready, 1)

            def tokens_lo(b):
                dve.wait_ge(lnhi_ready, b + 1)
                dve.tensor_tensor(ln_lo[:, :, :], lnf[:, :, :], ln_hi[:, :, :].bitcast(F32),
                                  ALU.subtract).then_inc(lnlo_ready, 1)

            def k_part(u, par, h):
                dve.wait_ge(khi_ready, u + 1)
                dve.scalar_tensor_tensor(out=k_lo[:, par, :], in0=ps_k[:, 0:KPAD], scalar=bkv[:, h:h + 1],
                                         in1=k_hi[:, par, :].bitcast(F32), op0=ALU.add,
                                         op1=ALU.subtract).then_inc(qklo_ready, 1)

            def q_part(u, par, h):
                dve.wait_ge(qhi_ready, u + 1)
                dve.scalar_tensor_tensor(out=q_lo[:, par, :], in0=ps_qa[:, 0:TOK], scalar=bqs[:, h:h + 1],
                                         in1=q_hi[:, par, :].bitcast(F32), op0=ALU.add,
                                         op1=ALU.subtract).then_inc(qklo_ready, 1)

            def v_piece(b, g):
                half, j = divmod(g, 3)
                rows = P if j < 2 else MEDIA
                dve.wait_ge(vhi_ready, VGROUPS * b + g + 1)
                dve.tensor_tensor(v_lo[0:rows, half, j, :], ps_v[0:rows, :], v_hi[0:rows, half, j, :].bitcast(F32),
                                  ALU.subtract).then_inc(vlo_ready, 1)

            def maximum(s, h, i):
                dve.wait_ge(scored, 2 * s + i + 1)
                _wait(dve, exp_ready, 2 * (s - 1))
                dve.tensor_reduce(nmax[:, h % 2, i:i + 1], ps_s[i][:, 0:KEYS], AX.X, ALU.max,
                                  negate=True).then_inc(max_ready, 1)

            def step(b, h):
                s = HEADS * b + h
                if _live(s, STEPS):
                    maximum(s, h, 0)
                if _live(s - 3, STEPS):
                    hh = (h - 3) % HEADS
                    dve.wait_ge(ohi_ready, s - 2)
                    dve.scalar_tensor_tensor(out=o_lo[:, (h - 3) % 2, :], in0=av(s - 3)[:, TOK:2 * TOK],
                                             scalar=bkv[:, HEADS + hh:HEADS + hh + 1],
                                             in1=o_hi[:, (h - 3) % 2, :].bitcast(F32), op0=ALU.add,
                                             op1=ALU.subtract).then_inc(olo_ready, 1)
                if _live(s, STEPS):
                    maximum(s, h, 1)
                if _live(s + 1, STEPS):
                    k_part(s + 1, (h + 1) % 2, (h + 1) % HEADS)
                if _live(s, STEPS):
                    if h == 1 and _live(b + 1, BATCH + 1):
                        dve.wait_ge(bn_ready, 3 * b + 4 + tiles(b + 1))
                        dve.wait_ge(rstd_ready, b + 1)
                    dve.wait_ge(exp_ready, 2 * s + 2)
                    _wait(dve, norm0_ready, s - 1)
                    dve.reciprocal(rinv[:, h % 2, :], rsum[:, h % 2, :]).then_inc(rinv_ready, 1)
                    if h == 1 and _live(b + 1, BATCH + 1):
                        aggregate(b + 1)
                if _live(s + 1, STEPS):
                    q_part(s + 1, (h + 1) % 2, (h + 1) % HEADS)
                if _live(s, STEPS):
                    dve.wait_ge(rinv_ready, s + 1)
                    dve.tensor_scalar(prob[:, h % 2, 1, 0:KEYS], prob[:, h % 2, 1, 0:KEYS], rinv[:, h % 2, 1:2], None,
                                      ALU.mult).then_inc(norm1_ready, 1)
                if h == 6 and _live(b + 1, BATCH):
                    tokens_lo(b + 1)
                if _live(s - 1, STEPS):
                    dve.wait_ge(pthi_ready, s)
                    dve.tensor_tensor(pt_lo[:, (h - 1) % 2, :], ps_t[:, 0:3 * TOK], pt_hi[:, (h - 1) % 2, :].bitcast(F32),
                                      ALU.subtract).then_inc(ptlo_ready, 1)
                bv = b + 1 if h == 7 else b
                if h in VG_AT and _live(bv, BATCH):
                    v_piece(bv, VG_AT[h])
                if h == 0 and _live(b + 1, BATCH + 1):
                    statistics(b + 1)
                if h == 4 and _live(b + 1, BATCH + 1):
                    normalise(b + 1)
                if h == 2 and _live(b - 1, BATCH):
                    rows = x_all[:, bass.ds(TT * (b - 1), TT), :]
                    dve.wait_ge(projected, HEADS * b)
                    dve.wait_ge(xb_ready, b)
                    dve.scalar_tensor_tensor(out=rows, in0=ps_y[:, :].rearrange("p (i d) -> p i d", i=TT),
                                             scalar=tg[:, 0:1], in1=rows, op0=ALU.mult,
                                             op1=ALU.add).then_inc(x2_ready, 1)

            dve.wait_ge(bn_ready, 1)
            statistics(0)
            dve.wait_ge(bn_ready, 4)
            aggregate(0)
            normalise(0)

            def split_lo(n):
                dve.wait_ge(whi_ready, n + 1)
                dve.scalar_tensor_tensor(out=piece(w_lo, n), in0=piece(raw, n), scalar=SCALE if PIECES[n][0] == 0 else 1.0,
                                         in1=piece(w_hi, n).bitcast(F32), op0=ALU.mult,
                                         op1=ALU.subtract).then_inc(wlo_ready, 1)

            split_lo(0)
            tokens_lo(0)
            split_lo(1)
            split_lo(2)
            k_part(0, 0, 0)
            q_part(0, 0, 0)
            v_piece(0, 0)
            for h in range(HEADS):
                step(0, h)
                for n in DVE_LO_AT.get(h, ()):
                    split_lo(n)
                if h == 0:
                    dve.wait_ge(tg_ready, 1)
                    dve.tensor_scalar(tgbo[:, :], bo[:, :], tg[:, 0:1], None, ALU.mult).then_inc(tg_ready, 1)
            with dve.Fori(1, BATCH - 1) as b:
                for h in range(HEADS):
                    step(b, h)
            for h in range(HEADS):
                step(BATCH - 1, h)
            for h in range(3):
                step(BATCH, h)

        @block.tensor
        def _(pe):
            def product(out, pairs, first=True, last=True):
                n = 0
                for s_hi, s_lo, m_hi, m_lo in pairs:
                    for a, m in ((s_hi, m_hi), (s_hi, m_lo), (s_lo, m_hi)):
                        n += 1
                        mm = pe.matmul(out, a, m, start=first and n == 1, stop=last and n == 3 * len(pairs))
                return mm

            def turn_tokens(b, c, bank=ps_v):
                pe.wait_ge(z_ready, 3 * (b + 1))
                if c == 0:
                    _wait(pe, vlo_ready, VGROUPS * b)
                elif bank is ps_v:
                    pe.wait_ge(tok_scaled, 2 * FC * b + 2)
                for i in range(TT):
                    pe.transpose(bank[:, i * P:(i + 1) * P], z[:, i, c * P:(c + 1) * P], ident[:, :])
                pe.transpose(bank[:, TOK:KEYS], z[0:MEDIA, 2, c * P:(c + 1) * P], ident[0:MEDIA, 0:MEDIA])\
                  .then_inc(tok_turned, 1)

            def project_qk(u, h, b):
                pe.wait_ge(lnlo_ready, b + 1)
                _wait(pe, qklo_ready, 2 * u - 1)
                product(ps_k[:, 0:KPAD], [(wk(w_hi, c, h), wk(w_lo, c, h), ln_hi[:, c, :], ln_lo[:, c, :])
                                          for c in range(FC)]).then_inc(qk_projected, 1)
                if isinstance(u, int) and u == 0:
                    pe.wait_ge(wlo_ready, 2)
                _wait(pe, qklo_ready, 2 * u)
                _wait(pe, olo_ready, u - 3)
                product(ps_qa[:, 0:TOK], [(wq(w_hi, c, h), wq(w_lo, c, h), ln_hi[:, c, 0:TOK], ln_lo[:, c, 0:TOK])
                                          for c in range(FC)]).then_inc(qk_projected, 1)

            def project_v(b, g):
                half, j = divmod(g, 3)
                if g == 0:
                    pe.wait_ge(tok_scaled, 2 * FC * (b + 1))
                else:
                    pe.wait_ge(vlo_ready, VGROUPS * b + g)
                j0, j1 = (j * P, (j + 1) * P) if j < 2 else (TOK, KEYS)
                product(ps_v[0:j1 - j0, :], [(ln_hi[:, c, j0:j1], ln_lo[:, c, j0:j1], wv(w_hi, c, half), wv(w_lo, c, half))
                                             for c in range(FC)]).then_inc(v_projected, 1)

            def project_out(b, h):
                s = HEADS * b + h
                hh = (h - 3) % HEADS
                par = (h - 3) % 2
                if isinstance(s, int) and s in (3, 7):
                    pe.wait_ge(wlo_pool, {3: 3, 7: 4}[s])
                pe.wait_ge(olo_ready, s - 2)
                if hh == 0:
                    _wait(pe, x2_ready, b)
                for i in range(TT):
                    for n, (a, m) in enumerate(((o_hi, w_hi), (o_hi, w_lo), (o_lo, w_hi))):
                        mm = pe.matmul(ps_y[:, i * DIM:(i + 1) * DIM], a[:, par, i * P:(i + 1) * P], wo(m, hh),
                                       start=hh == 0 and i == 0 and n == 0, stop=hh == HEADS - 1 and n == 2,
                                       skip_group_check=True)
                mm.then_inc(projected, 1)

            def attend(b, h):
                s = HEADS * b + h
                hh = (h - 2) % HEADS
                bw = b if h >= 2 else b - 1
                half, col = hh // 4, (hh % 4) * DH
                pe.wait_ge(ptlo_ready, s - 1)
                pe.wait_ge(vlo_ready, VGROUPS * bw + 3 * (half + 1))
                if _live(s + 1, STEPS):
                    pe.wait_ge(qklo_ready, 2 * (s + 2))
                if av(s - 2) is ps_qa:
                    _wait(pe, olo_ready, s - 2)
                else:
                    pe.wait_ge(qklo_ready, 2 * STEPS)
                product(av(s - 2)[:, TOK:2 * TOK], [
                    (v_hi[0:r, half, j, col:col + DH], v_lo[0:r, half, j, col:col + DH],
                     pt_hi[0:r, h % 2, j * TOK:(j + 1) * TOK], pt_lo[0:r, h % 2, j * TOK:(j + 1) * TOK])
                    for j, r in enumerate((P, P, MEDIA))]).then_inc(attended, 1)

            def step(b, h):
                s = HEADS * b + h
                if _live(s, STEPS):
                    pe.wait_ge(qklo_ready, 2 * (s + 1))
                    for i in range(TT):
                        _wait(pe, exp_ready, 2 * s - 1 + i)
                        product(ps_s[i][:, 0:KPAD], [(q_hi[:, h % 2, i * P:(i + 1) * P], q_lo[:, h % 2, i * P:(i + 1) * P],
                                                      k_hi[:, h % 2, :], k_lo[:, h % 2, :])]).then_inc(scored, 1)
                if isinstance(s, int) and s == 3:
                    pe.wait_ge(wlo_pool, 2)
                    pe.wait_ge(wlo_ready, 4)
                if _live(s + 1, STEPS):
                    project_qk(s + 1, (h + 1) % HEADS, b + 1 if h == HEADS - 1 else b)
                if _live(s - 1, STEPS):
                    if isinstance(s, int) and s == 1:
                        pe.wait_ge(const_ready, 2)
                    pe.wait_ge(norm0_ready, s)
                    pe.wait_ge(norm1_ready, s)
                    _wait(pe, ptlo_ready, s - 1)
                    for j in range(3):
                        j0, j1 = (j * P, (j + 1) * P) if j < 2 else (TOK, KEYS)
                        for i in range(TT):
                            mm = pe.transpose(ps_t[0:j1 - j0, j * TOK + i * P:j * TOK + (i + 1) * P],
                                              prob[:, (h - 1) % 2, i, j0:j1], ident[:, :])
                    mm.then_inc(p_turned, 1)
                bv = b + 1 if h == 7 else b
                if isinstance(b, int) and b == 0 and h == 2:
                    pe.wait_ge(wlo_pool, 1)
                if h in VG_AT and _live(bv, BATCH):
                    project_v(bv, VG_AT[h])
                if h == 5 and _live(b + 1, BATCH):
                    turn_tokens(b + 1, 0)
                last = isinstance(s, int) and s - 2 == STEPS - 1
                if last:
                    attend(b, h)
                if _live(s - 3, STEPS):
                    project_out(b, h)
                if _live(s - 2, STEPS) and not last:
                    attend(b, h)
                if h == 5 and _live(b + 1, BATCH):
                    turn_tokens(b + 1, 1)

            pe.wait_ge(id_ready, 2)
            pe.wait_ge(rows_in, 16 * 6)
            pe.transpose(ps_y[:, 0:VR], vec_rows[:, :], ident[0:VR, 0:VR]).then_inc(rows_turned, 1)
            for c, bank in enumerate((ps_v, ps_k)):
                turn_tokens(0, c, bank)
            pe.wait_ge(wlo_ready, 1)
            project_qk(0, 0, 0)
            pe.wait_ge(wlo_ready, 3)
            project_v(0, 0)
            for h in range(HEADS):
                step(0, h)
            with pe.Fori(1, BATCH - 1) as b:
                for h in range(HEADS):
                    step(b, h)
            for h in range(HEADS):
                step(BATCH - 1, h)
            for h in range(3):
                step(BATCH, h)


def ffn(nc, t, x_all, ident, z, raw_gu, raw_down, raw_in):
    with ExitStack() as ctx:
        def sb(name, shape, dt=F32):
            return ctx.enter_context(nc.sbuf_tensor(name, shape, dt))

        def ps(name, shape):
            return ctx.enter_context(nc.psum_tensor(name, shape, F32))

        def sem(name):
            return ctx.enter_context(nc.semaphore(name))

        UNIT = (EXP,) + tuple(range(EXP))
        NU = len(UNIT)
        LEAD = 4
        RING = 3
        TURN_AT, COMB_AT = 5, 7
        WEIGH_LAG, LO_LAG, DOWN_LAG, OUT_LAG = NU + 3, NU + 4, NU + 5, NU + 6

        gu_hi = sb("gu_hi", [P, FC, GU - EXP], F32R)
        gu_lo = sb("gu_lo", [P, FC, GU - EXP], F32R)
        dn_hi = sb("dn_hi", [P, EXP + 1, DIM], F32R)
        dn_lo = sb("dn_lo", [P, EXP + 1, DIM], F32R)
        router = sb("router", [P, FC, 2 * EXP], F32R)
        logits = sb("logits", [P, TT, EXP])
        gf = sb("gf", [P, 1])
        tgf = sb("tgf", [P, 1])
        bias = sb("bias", [P, EXP])
        bias_half = sb("bias_half", [P, EXP])
        before = sb("before", [P, EXP, EXP])
        mhalf2 = sb("mhalf2", [P, TT])
        eps2 = sb("eps2", [P, TT])
        stats2 = sb("stats2", [P, TT, 6])
        mv2 = sb("mv2", [P, TT, 2])
        rstd = sb("rstd", [P, 2, TT])
        xt_hi = sb("xt_hi", [P, 2, FC, TOK], F32R)
        xt_lo = sb("xt_lo", [P, 2, FC, TOK], F32R)
        th = sb("th", [P, RING, TOK])
        act_a = sb("act_a", [P, RING, TOK])
        act_h = sb("act_h", [P, 2, NU, TOK])
        f_hi = sb("f_hi", [P, RING, TOK], F32R)
        f_lo = sb("f_lo", [P, RING, TOK], F32R)
        tl = sb("tl", [P, TT, EXP])
        comb = sb("comb", [P, TT, EXP])
        comb_t = sb("comb_t", [EXP, TOK])
        wide_w = sb("wide_w", [P, 2, EXP, TOK])
        half_w = sb("half_w", [P, TOK])
        sig = sb("sig", [P, TT, EXP + 1])
        choice = sb("choice", [P, 2 * TT, 4])
        sums6 = sb("sums6", [P, 2 * TT, 6])
        gsum = sb("gsum", [P, 2 * TT])
        pick = sb("pick", [P, 2 * TT])
        cmp_both = sb("cmp_both", [P, TT * EXP, 2 * EXP])
        rank = sb("rank", [P, TT * EXP])
        wsum = sb("wsum", [P, 2, TT])
        y_out = sb("y_out", [P, TT, DIM])
        comb_dram = nc.dram_tensor("comb_rows", [PAIRS, EXP, TOK], F32, kind="Internal").ap()

        ps_gu = [ps(f"ps_gu{n}", [P, 512]) for n in range(RING)]
        ps_x = ps("ps_x", [P, 512])
        ps_r = ps("ps_r", [P, 512])
        ps_o = [ps("ps_o0", [P, 512]), ps("ps_o1", [P, 512])]

        vec_in, ffn_gate, wsplit_hi, wsplit_lo = sem("f_vec_in"), sem("f_gate"), sem("f_wsplit_hi"), sem("f_wsplit_lo")
        dnlo_ready = sem("f_dnlo")
        masks, half2, consts = sem("f_masks"), sem("f_half"), sem("f_consts")
        bn2, var_ready, rstep, rstd_ready, z_ready = sem("f_bn"), sem("f_var"), sem("f_rstep"), sem("f_rstd"), sem("f_z")
        x_turned, xthi_ready, xtlo_ready = sem("f_x_turned"), sem("f_xthi"), sem("f_xtlo")
        gu_done, tanh_done, a_done, h_done = sem("f_gu_done"), sem("f_tanh"), sem("f_a"), sem("f_h")
        router_hi, router_lo, logits_hi, logits_ready = sem("f_router_hi"), sem("f_router_lo"), sem("f_logits_hi"), sem("f_logits")
        routed, logit_tanh, comb_ready, route = sem("f_routed"), sem("f_logit_tanh"), sem("f_comb"), sem("f_route")
        comb_turned, combt_ready, comb_out, wide_in = sem("f_comb_turned"), sem("f_combt"), sem("f_comb_out"), sem("f_wide_in")
        f_ready, fhi_ready, flo_ready = sem("f_f"), sem("f_fhi"), sem("f_flo")
        f_last = sem("f_last")
        flo_late = sem("f_flo_late")
        down_done, y_ready, y_stored = sem("f_down"), sem("f_y"), sem("f_y_stored")

        GU_PIECES = 1 + EXP // 2
        NEEDS = {0: 1, 1: 2, 3: 3, 5: 4, 7: 5}
        ROUTE_STEPS = 16

        def gu_piece(w, n):
            if n == 0:
                return w[:, :, 2048:GU - EXP]
            half, two = divmod(n - 1, 2)
            return w[:, :, half * 1024:(half + 1) * 1024].rearrange("p c (k n) -> p c k n", k=2)\
                [:, :, :, two * 256:(two + 1) * 256]

        def columns(e):
            if e == EXP:
                return 2048, 2048 + I
            c0 = e // 4 * 1024 + e % 4 * I
            return c0, c0 + 512

        def lagged(p, par, n, lag):
            back = (n - lag) // NU
            return p + back, (par + back) % 2, (n - lag) % NU

        LATE = [lagged(PAIRS, 0, n, LO_LAG) for n in range(LO_LAG)]

        block = ctx.enter_context(nc.Block())

        @block.sync
        def _(sp):
            sp.dma_start(gf[:, :], t["g_ffn"].unsqueeze(0).to_broadcast([P, 1])).then_inc(vec_in, 16)
            sp.dma_start(bias[:, :], t["L0_ffn_correction_bias"].unsqueeze(0).to_broadcast([P, EXP])).then_inc(vec_in, 16)
            out = t["out"].rearrange("b (i p) d -> b p i d", p=P)

            def store(p):
                sp.wait_ge(y_ready, p + 1)
                sp.dma_start(out[bass.ds(p, 1)].rearrange("o p i d -> (o p) i d"), y_out[:, :, :]).then_inc(y_stored, 16)

            def widen(p, par):
                sp.wait_ge(combt_ready, p + 1)
                sp.dma_start(comb_dram[bass.ds(p, 1)].rearrange("o e n -> (o e) n"), comb_t[:, :]).then_inc(comb_out, 16)
                sp.wait_ge(comb_out, 16 * (p + 1))
                sp.dma_start(wide_w[:, par, :, :], comb_dram[bass.ds(p, 1)].to_broadcast([P, EXP, TOK])).then_inc(wide_in, 16)

            widen(0, 0)
            widen(1, 1)
            def pair(p, par):
                store(p - 2)
                widen(p, par)

            with sp.Fori(2, PAIRS - 2, 2) as p:
                pair(p, 0)
                pair(p + 1, 1)
            pair(PAIRS - 2, 0)
            pair(PAIRS - 1, 1)
            store(PAIRS - 2)
            store(PAIRS - 1)
            sp.wait_ge(y_stored, 16 * PAIRS)

        @block.gpsimd
        def _(pool):
            pool.memset(mhalf2[:, :], -0.5).then_inc(half2, 1)
            pool.memset(eps2[:, :], EPS).then_inc(half2, 1)
            pool.memset(before[:, :, :], 1.0).then_inc(masks, 1)
            pool.memset(half_w[:, :], 0.5).then_inc(masks, 1)
            pool.wait_ge(masks, 2)
            pool.affine_select(out=before[:, :, :], in_=before[:, :, :], compare_op=ALU.is_gt, fill=0.0, base=0,
                               pattern=[[1, EXP], [-1, EXP]], channel_multiplier=0).then_inc(masks, 1)

            def reciprocal_deviation(p):
                pool.wait_ge(var_ready, TT * p)
                _wait(pool, z_ready, TT * (p - 1))
                pool.wait_ge(half2, 2)
                pool.tensor_tensor(rstd[:, 0, :], mv2[:, :, 1], eps2[:, :], ALU.add).then_inc(rstep, 1)
                pool.wait_ge(rstep, p)
                pool.tensor_tensor(rstd[:, 1, :], rstd[:, 0, :], mhalf2[:, :], ALU.pow).then_inc(rstd_ready, 1)

            def weigh(p, par, m):
                pool.wait_ge(h_done, NU * p + m + 1)
                if m == 1:
                    pool.wait_ge(wide_in, 16 * (p + 1))
                row = half_w[:, :] if m == 0 else wide_w[:, par, UNIT[m], :]
                pool.tensor_tensor(act_h[:, par, m, :], act_h[:, par, m, :], row, ALU.mult).then_inc(f_ready, 1)

            def low_part(p, par, m):
                pool.wait_ge(fhi_ready, NU * p + m + 1)
                pool.tensor_tensor(f_lo[:, m % RING, :], act_h[:, par, m, :], f_hi[:, m % RING, :].bitcast(F32),
                                   ALU.subtract).then_inc(flo_ready, 1)

            def pair(p, par):
                for n in range(NU):
                    q, qpar, m = lagged(p, par, n, WEIGH_LAG)
                    if _live(q, PAIRS):
                        weigh(q, qpar, m)
                    q, qpar, m = lagged(p, par, n, LO_LAG)
                    if _live(q, PAIRS):
                        low_part(q, qpar, m)
                    if n == 2 and _live(p + 1, PAIRS):
                        reciprocal_deviation(p + 1)

            pool.wait_ge(wsplit_hi, FC * GU_PIECES + 1)
            pool.tensor_tensor(dn_lo[:, :, :], raw_down[:, :, :], dn_hi[:, :, :].bitcast(F32),
                               ALU.subtract).then_inc(dnlo_ready, 1)
            for p in range(LEAD):
                pair(p, p % 2)
            with pool.Fori(LEAD, PAIRS - 2, 2) as p:
                pair(p, 0)
                pair(p + 1, 1)
            pair(PAIRS - 2, 0)
            pair(PAIRS - 1, 1)
            for n in range(WEIGH_LAG - NU):
                weigh(*lagged(PAIRS, 0, n, WEIGH_LAG))

        @block.scalar
        def _(act):
            def tokens_hi(p, par):
                act.wait_ge(x_turned, p + 1)
                _wait(act, gu_done, NU * (p - 1))
                act.activation(xt_hi[:, par, :, :].rearrange("p c n -> p (c n)"), ps_x[:, :], ACT.Copy).then_inc(xthi_ready, 1)

            def high_part(p, par, m):
                if isinstance(p, int) and p == PAIRS - 1:
                    act.wait_ge(f_last, m + 1)
                else:
                    act.wait_ge(f_ready, NU * p + m + 1)
                _wait(act, down_done, NU * p + m + 1 - RING)
                act.activation(f_hi[:, m % RING, :], act_h[:, par, m, :], ACT.Copy).then_inc(fhi_ready, 1)

            def pair(p, par):
                for n in range(NU):
                    act.wait_ge(gu_done, NU * p + n + 1)
                    _wait(act, a_done, NU * p + n + 1 - RING)
                    act.activation(th[:, n % RING, :], ps_gu[n % RING][:, 0:TOK], ACT.Tanh, scale=0.5).then_inc(tanh_done, 1)
                    if n == 1:
                        act.wait_ge(logits_ready, p + 1)
                        _wait(act, comb_ready, p)
                        act.activation(tl[:, :, :], logits[:, :, :], ACT.Tanh, scale=0.5).then_inc(logit_tanh, 1)
                    if n == TURN_AT and _live(p + 1, PAIRS):
                        tokens_hi(p + 1, 1 - par)
                    if n == COMB_AT:
                        act.wait_ge(comb_turned, p + 1)
                        _wait(act, comb_out, 16 * p)
                        act.activation(comb_t[:, :], ps_r[0:EXP, TOK:2 * TOK], ACT.Copy).then_inc(combt_ready, 1)
                    q, qpar, m = lagged(p, par, n, WEIGH_LAG)
                    if _live(q, PAIRS):
                        high_part(q, qpar, m)

            act.wait_ge(raw_in, 16 * RAW_DMAS)
            raw_router = raw_gu[:, :, GU - EXP:GU]
            act.activation(router[:, :, 0:EXP], raw_router, ACT.Copy).then_inc(router_hi, 1)
            for n in range(GU_PIECES):
                for c in range(FC):
                    act.activation(gu_piece(gu_hi, n)[:, c], gu_piece(raw_gu, n)[:, c], ACT.Copy).then_inc(wsplit_hi, 1)
                if n == 0:
                    tokens_hi(0, 0)
            act.activation(dn_hi[:, :, :], raw_down[:, :, :], ACT.Copy).then_inc(wsplit_hi, 1)
            act.wait_ge(vec_in, 32)
            act.activation(tgf[:, :], gf[:, :], ACT.Tanh).then_inc(ffn_gate, 1)
            for p in range(LEAD):
                pair(p, p % 2)
            with act.Fori(LEAD, PAIRS - 2, 2) as p:
                pair(p, 0)
                pair(p + 1, 1)
            pair(PAIRS - 2, 0)
            pair(PAIRS - 1, 1)
            for n in range(WEIGH_LAG):
                high_part(*lagged(PAIRS, 0, n, WEIGH_LAG))

        @block.vector
        def _(dve):
            def statistics(p):
                for i in range(TT):
                    dve.bn_stats(stats2[:, i, :], x_all[:, bass.ds(TT * p + i, 1), :].rearrange("p o d -> p (o d)"))\
                       .then_inc(bn2, 1)

            def aggregate(p):
                for i in range(TT):
                    dve.bn_aggr(mv2[:, i, :], stats2[:, i, :]).then_inc(var_ready, 1)

            def normalise(p):
                dve.wait_ge(rstd_ready, p)
                _wait(dve, x_turned, p)
                for i in range(TT):
                    dve.tensor_scalar(z[:, i, :], x_all[:, bass.ds(TT * p + i, 1), :].rearrange("p o d -> p (o d)"),
                                      mv2[:, i, 0:1], rstd[:, 1, i:i + 1], ALU.subtract, ALU.mult).then_inc(z_ready, 1)

            def tokens_lo(p, par):
                dve.wait_ge(xthi_ready, p + 1)
                dve.tensor_tensor(xt_lo[:, par, :, :].rearrange("p c n -> p (c n)"), ps_x[:, :],
                                  xt_hi[:, par, :, :].rearrange("p c n -> p (c n)").bitcast(F32),
                                  ALU.subtract).then_inc(xtlo_ready, 1)

            def output(p, par):
                dve.wait_ge(down_done, NU * (p + 1))
                _wait(dve, y_stored, 16 * p)
                if isinstance(p, int) and p == 0:
                    dve.wait_ge(ffn_gate, 1)
                dve.scalar_tensor_tensor(out=y_out[:, :, :], in0=ps_o[par][:, :].rearrange("p (i d) -> p i d", i=TT),
                                         scalar=tgf[:, 0:1], in1=x_all[:, bass.ds(TT * p, TT), :],
                                         op0=ALU.mult, op1=ALU.add).then_inc(y_ready, 1)

            flat = choice[:, :, :].rearrange("p a b -> p (a b)")
            by_tile = flat.rearrange("p (i e) -> p i e", i=TT)
            scores = sig[:, :, 0:EXP]
            both = cmp_both[:, :, :].rearrange("p (i e) n -> p i e n", i=TT)

            def sum_logits(p):
                dve.wait_ge(routed, p + 1)
                _wait(dve, logit_tanh, p)
                both_parts = ps_r[:, 0:TT * 2 * EXP].rearrange("p (i n) -> p i n", i=TT)
                dve.tensor_copy(logits[:, :, :], both_parts[:, :, 0:EXP]).then_inc(logits_hi, 1)
                dve.wait_ge(logits_hi, p + 1)
                dve.tensor_tensor(logits[:, :, :], logits[:, :, :], both_parts[:, :, EXP:], ALU.add).then_inc(logits_ready, 1)

            def choices(p):
                dve.wait_ge(logit_tanh, p + 1)
                _wait(dve, comb_ready, p)
                dve.scalar_tensor_tensor(out=by_tile, in0=tl[:, :, :], scalar=0.5,
                                         in1=bias_half[:, :].unsqueeze(1).to_broadcast([P, TT, EXP]),
                                         op0=ALU.mult, op1=ALU.add).then_inc(route, 1)
                dve.tensor_scalar(scores, tl[:, :, :], 0.5, 0.5, ALU.mult, ALU.add).then_inc(route, 1)

            def pair_sums(p):
                dve.wait_ge(route, ROUTE_STEPS * p + 2)
                dve.tensor_tensor(sums6[:, :, 0:3], choice[:, :, 0:3], choice[:, :, 1:4], ALU.add).then_inc(route, 1)
                dve.tensor_tensor(sums6[:, :, 3:5], choice[:, :, 0:2], choice[:, :, 2:4], ALU.add).then_inc(route, 1)
                dve.tensor_tensor(sums6[:, :, 5:6], choice[:, :, 0:1], choice[:, :, 3:4], ALU.add).then_inc(route, 1)

            def group_sums(p):
                dve.wait_ge(route, ROUTE_STEPS * p + 5)
                dve.tensor_reduce(gsum[:, :], sums6[:, :, :], AX.X, ALU.max).then_inc(route, 1)

            def pick_group(p):
                dve.wait_ge(route, ROUTE_STEPS * p + 6)
                g = gsum[:, :].rearrange("p (i g) -> p i g", g=2)
                picks = pick[:, :].rearrange("p (i g) -> p i g", g=2)
                dve.tensor_tensor(picks[:, :, 0], g[:, :, 0], g[:, :, 1], ALU.is_ge).then_inc(route, 1)
                dve.tensor_tensor(picks[:, :, 1], g[:, :, 1], g[:, :, 0], ALU.is_gt).then_inc(route, 1)

            def mask_choices(p):
                dve.wait_ge(route, ROUTE_STEPS * p + 8)
                dve.tensor_tensor(choice[:, :, :], choice[:, :, :], pick[:, :].unsqueeze(2).to_broadcast([P, 2 * TT, 4]),
                                  ALU.mult).then_inc(route, 1)

            def compare(p):
                dve.wait_ge(route, ROUTE_STEPS * p + 9)
                other = by_tile.unsqueeze(2).to_broadcast([P, TT, EXP, EXP])
                own = by_tile.unsqueeze(3).to_broadcast([P, TT, EXP, EXP])
                dve.tensor_tensor(both[:, :, :, 0:EXP], other, own, ALU.is_gt).then_inc(route, 1)
                dve.tensor_tensor(both[:, :, :, EXP:], other, own, ALU.is_equal).then_inc(route, 1)

            def break_ties(p):
                dve.wait_ge(route, ROUTE_STEPS * p + 11)
                dve.tensor_tensor(both[:, :, :, EXP:], both[:, :, :, EXP:],
                                  before[:, :, :].unsqueeze(1).to_broadcast([P, TT, EXP, EXP]), ALU.mult).then_inc(route, 1)

            def ranks(p):
                dve.wait_ge(route, ROUTE_STEPS * p + 12)
                dve.tensor_reduce(rank[:, :], cmp_both[:, :, :], AX.X, ALU.add).then_inc(route, 1)

            def select_scores(p):
                dve.wait_ge(route, ROUTE_STEPS * p + 13)
                dve.scalar_tensor_tensor(out=scores, in0=rank[:, :].rearrange("p (i e) -> p i e", i=TT), scalar=2.0,
                                         in1=scores, op0=ALU.is_lt, op1=ALU.mult).then_inc(route, 1)

            def score_sum(p):
                dve.wait_ge(route, ROUTE_STEPS * p + 14)
                dve.tensor_reduce(wsum[:, 0, :], sig[:, :, :], AX.X, ALU.add).then_inc(route, 1)

            def invert_sum(p):
                dve.wait_ge(route, ROUTE_STEPS * p + 15)
                dve.reciprocal(wsum[:, 1, :], wsum[:, 0, :]).then_inc(route, 1)

            def weights(p):
                dve.wait_ge(route, ROUTE_STEPS * p + 16)
                _wait(dve, comb_turned, p)
                dve.scalar_tensor_tensor(out=comb[:, :, :], in0=scores, scalar=0.5,
                                         in1=wsum[:, 1, :].unsqueeze(2).to_broadcast([P, TT, EXP]),
                                         op0=ALU.mult, op1=ALU.mult).then_inc(comb_ready, 1)

            ROUTING = {0: ((), (sum_logits,)),
                       1: ((), (choices,)),
                       2: ((pair_sums,), (group_sums,)),
                       3: ((pick_group,), (mask_choices,)),
                       4: ((compare,), (break_ties,)),
                       5: ((ranks,), (select_scores,)),
                       6: ((score_sum,), (invert_sum, weights))}

            def pair(p, par):
                for n in range(NU):
                    bank = ps_gu[n % RING]
                    if n == TURN_AT + 1 and _live(p + 1, PAIRS):
                        tokens_lo(p + 1, 1 - par)
                    if n == 4 and _live(p + 1, PAIRS):
                        normalise(p + 1)
                    if n == 1 and _live(p + 1, PAIRS):
                        dve.wait_ge(bn2, TT * (p + 1))
                        _wait(dve, rstd_ready, p)
                    dve.wait_ge(tanh_done, NU * p + n + 1)
                    _wait(dve, h_done, NU * p + n + 1 - RING)
                    dve.scalar_tensor_tensor(out=act_a[:, n % RING, :], in0=th[:, n % RING, :], scalar=1.0,
                                             in1=bank[:, 0:TOK], op0=ALU.add, op1=ALU.mult).then_inc(a_done, 1)
                    if n == 1 and _live(p + 1, PAIRS):
                        aggregate(p + 1)
                    for routing in ROUTING.get(n, ((), ()))[0]:
                        routing(p)
                    dve.wait_ge(a_done, NU * p + n + 1)
                    _wait(dve, flo_ready, NU * (p - 2) + n + 1)
                    dve.tensor_tensor(act_h[:, par, n, :], act_a[:, n % RING, :], bank[:, TOK:2 * TOK],
                                      ALU.mult).then_inc(h_done, 1)
                    for routing in ROUTING.get(n, ((), ()))[1]:
                        routing(p)
                    q, qpar, m = lagged(p, par, n, OUT_LAG)
                    if m == NU - 1 and _live(q, PAIRS):
                        output(q, qpar)
                    if n == 0 and _live(p + 1, PAIRS):
                        statistics(p + 1)

            def split_lo(n):
                dve.wait_ge(wsplit_hi, FC * (n + 1))
                for c in range(FC):
                    dve.tensor_tensor(gu_piece(gu_lo, n)[:, c], gu_piece(raw_gu, n)[:, c],
                                      gu_piece(gu_hi, n)[:, c].bitcast(F32), ALU.subtract).then_inc(wsplit_lo, 1)

            dve.memset(sig[:, :, EXP:EXP + 1], 1e-20).then_inc(consts, 1)
            dve.wait_ge(router_hi, 1)
            dve.tensor_tensor(router[:, :, EXP:], raw_gu[:, :, GU - EXP:GU], router[:, :, 0:EXP].bitcast(F32),
                              ALU.subtract).then_inc(router_lo, 1)
            split_lo(0)
            tokens_lo(0, 0)
            for n in range(1, GU_PIECES):
                split_lo(n)
            dve.wait_ge(vec_in, 32)
            dve.tensor_scalar(bias_half[:, :], bias[:, :], 0.5, None, ALU.add).then_inc(consts, 1)
            dve.wait_ge(consts, 2)
            dve.wait_ge(masks, 3)
            for p in range(LEAD):
                pair(p, p % 2)
            with dve.Fori(LEAD, PAIRS - 2, 2) as p:
                pair(p, 0)
                pair(p + 1, 1)
            pair(PAIRS - 2, 0)
            pair(PAIRS - 1, 1)
            for n, (q, qpar, m) in enumerate(LATE):
                if n + 1 < len(LATE) and LATE[n + 1][0] == PAIRS - 1:
                    k = LATE[n + 1][2]
                    if k == 1:
                        dve.wait_ge(wide_in, 16 * PAIRS)
                    row = half_w[:, :] if k == 0 else wide_w[:, 1, UNIT[k], :]
                    dve.wait_ge(h_done, NU * (PAIRS - 1) + k + 1)
                    dve.tensor_tensor(act_h[:, 1, k, :], act_h[:, 1, k, :], row, ALU.mult).then_inc(f_last, 1)
                dve.wait_ge(fhi_ready, NU * q + m + 1)
                dve.tensor_tensor(f_lo[:, m % RING, :], act_h[:, qpar, m, :], f_hi[:, m % RING, :].bitcast(F32),
                                  ALU.subtract).then_inc(flo_late, 1)
                if q == PAIRS - 1 and m == 0:
                    output(PAIRS - 2, 0)
            output(PAIRS - 1, 1)

        @block.tensor
        def _(pe):
            def turn_tokens(p):
                _wait(pe, z_ready, TT * p)
                _wait(pe, xtlo_ready, p)
                for c in range(FC):
                    for i in range(TT):
                        mm = pe.transpose(ps_x[:, c * TOK + i * P:c * TOK + (i + 1) * P], z[:, i, c * P:(c + 1) * P], ident[:, :])
                mm.then_inc(x_turned, 1)

            def gate_up(p, par, n):
                _wait(pe, h_done, NU * p + n + 1 - RING)
                if n == 0:
                    pe.wait_ge(xtlo_ready, p + 1)
                if isinstance(p, int) and p == 0 and n in NEEDS:
                    pe.wait_ge(wsplit_lo, FC * NEEDS[n])
                for k, c0 in enumerate(columns(UNIT[n])):
                    first = True
                    for c in range(FC):
                        for w, x in ((gu_hi, xt_hi), (gu_hi, xt_lo), (gu_lo, xt_hi)):
                            mm = pe.matmul(ps_gu[n % RING][:, k * TOK:(k + 1) * TOK], w[:, c, c0:c0 + I], x[:, par, c, :],
                                           start=first, stop=c == FC - 1 and w is gu_lo)
                            first = False
                mm.then_inc(gu_done, 1)

            def route(p, par):
                _wait(pe, combt_ready, p)
                if isinstance(p, int) and p == 0:
                    pe.wait_ge(router_lo, 1)
                for i in range(TT):
                    for c in range(FC):
                        for x in (xt_hi, xt_lo):
                            mm = pe.matmul(ps_r[:, i * 2 * EXP:(i + 1) * 2 * EXP], x[:, par, c, i * P:(i + 1) * P],
                                           router[:, c, :], start=c == 0 and x is xt_hi, stop=c == FC - 1 and x is xt_lo)
                mm.then_inc(routed, 1)

            def turn_weights(p):
                pe.wait_ge(comb_ready, p + 1)
                for i in range(TT):
                    mm = pe.transpose(ps_r[0:EXP, TOK + i * P:TOK + (i + 1) * P], comb[:, i, :], ident[:, :])
                mm.then_inc(comb_turned, 1)

            def down(p, par, m):
                if isinstance(p, int) and (p, par, m) in LATE:
                    pe.wait_ge(flo_late, LATE.index((p, par, m)) + 1)
                else:
                    pe.wait_ge(flo_ready, NU * p + m + 1)
                if m == 0:
                    _wait(pe, y_ready, p - 1)
                for i in range(TT):
                    for k, (a, wd) in enumerate(((f_hi, dn_hi), (f_hi, dn_lo), (f_lo, dn_hi))):
                        mm = pe.matmul(ps_o[par][:, i * DIM:(i + 1) * DIM], a[:, m % RING, i * P:(i + 1) * P],
                                       wd[:, UNIT[m], :], start=m == 0 and i == 0 and k == 0,
                                       stop=m == NU - 1 and k == 2, skip_group_check=True)
                mm.then_inc(down_done, 1)

            def pair(p, par):
                for n in range(NU):
                    gate_up(p, par, n)
                    if n == 0:
                        route(p, par)
                    if n == TURN_AT and _live(p + 1, PAIRS):
                        turn_tokens(p + 1)
                    if n == COMB_AT:
                        turn_weights(p)
                    q, qpar, m = lagged(p, par, n, DOWN_LAG)
                    if _live(q, PAIRS):
                        if isinstance(q, int) and q == 0 and m == 0:
                            pe.wait_ge(dnlo_ready, 1)
                        down(q, qpar, m)

            turn_tokens(0)
            for p in range(LEAD):
                pair(p, p % 2)
            with pe.Fori(LEAD, PAIRS - 2, 2) as p:
                pair(p, 0)
                pair(p + 1, 1)
            pair(PAIRS - 2, 0)
            pair(PAIRS - 1, 1)
            for n in range(DOWN_LAG):
                down(*lagged(PAIRS, 0, n, DOWN_LAG))


def load_ffn_weights(engine, t, raw_gu, raw_down, raw_in):
    for c in range(FC):
        rows = slice(c * P, (c + 1) * P)
        for half in range(2):
            for k, name in enumerate(("w_gate", "w_up")):
                engine.dma_start(raw_gu[:, c, half * 1024 + k * 512:half * 1024 + (k + 1) * 512].rearrange("p (e i) -> p e i", e=4),
                                 t["L0_ffn_" + name][half * 4:half * 4 + 4, rows, :].rearrange("e p i -> p e i")).then_inc(raw_in, 16)
    for k, name in enumerate(("sw_gate", "sw_up")):
        engine.dma_start(raw_gu[:, :, 2048 + k * I:2048 + (k + 1) * I],
                         t["L0_ffn_" + name].rearrange("(c p) i -> p c i", p=P)).then_inc(raw_in, 16)
    engine.dma_start(raw_down[:, 0:EXP, :], t["L0_ffn_w_down"].rearrange("e p d -> p e d")).then_inc(raw_in, 16)
    engine.dma_start(raw_down[:, EXP, :], t["L0_ffn_sw_down"]).then_inc(raw_in, 16)
    for c in range(FC):
        engine.dma_start(raw_gu[:, c, 2048 + 2 * I:GU],
                         t["L0_ffn_router_weight"][:, c * P:(c + 1) * P].rearrange("e p -> p e"),
                         allow_slow_non_contiguous=True).then_inc(raw_in, 16)


def build(nc, t):
    with ExitStack() as ctx:
        x_all = ctx.enter_context(nc.sbuf_tensor("x_all", [P, TT * BATCH, DIM], F32))
        ident = ctx.enter_context(nc.sbuf_tensor("ident", [P, P], F32))
        z = ctx.enter_context(nc.sbuf_tensor("z", [P, 3, DIM], F32))
        raw = ctx.enter_context(nc.sbuf_tensor("raw", [P, RAW], F32))
        raw_in = ctx.enter_context(nc.semaphore("raw_in"))
        raw_gu = raw[:, 0:FC * GU].rearrange("p (c n) -> p c n", c=FC)
        raw_down = raw[:, FC * GU:FC * GU + (EXP + 1) * DIM].rearrange("p (e d) -> p e d", e=EXP + 1)
        attention(nc, t, x_all, ident, z, raw, lambda engine: load_ffn_weights(engine, t, raw_gu, raw_down, raw_in))
        ffn(nc, t, x_all, ident, z, raw_gu, raw_down, raw_in)


_INS = ['x', 'ctx_1024', 'g_xattn', 'g_ffn', 'L0_xattn_gamma_media', 'L0_xattn_beta_media', 'L0_xattn_gamma_lat',
        'L0_xattn_beta_lat', 'L0_xattn_Wq', 'L0_xattn_bq', 'L0_xattn_Wkv', 'L0_xattn_bkv', 'L0_xattn_Wo', 'L0_xattn_bo',
        'L0_ffn_router_weight', 'L0_ffn_correction_bias', 'L0_ffn_w_gate', 'L0_ffn_w_up', 'L0_ffn_w_down',
        'L0_ffn_sw_gate', 'L0_ffn_sw_up', 'L0_ffn_sw_down']


def kernel(**inputs):
    import numpy as _np
    import concourse.bacc as _bacc
    from concourse import mybir as _mybir
    from concourse.bass_utils import run_bass_kernel_spmd as _run

    nc = _bacc.Bacc("TRN2", target_bir_lowering=False, num_devices=1)
    arrays, t = {}, {}
    for name in _INS:
        a = _np.ascontiguousarray(inputs[name])
        arrays[f"in_{name}_dram"] = a
        t[name] = nc.dram_tensor(f"in_{name}_dram", a.shape, _mybir.dt.from_np(a.dtype), kind="ExternalInput").ap()
    t["out"] = nc.dram_tensor("out_0_dram", (BATCH, TOK, DIM), F32, kind="ExternalOutput").ap()
    build(nc, t)
    r = _run(nc, [arrays], core_ids=[0])
    return r.results[0]["out_0_dram"]
```
